# Optimizing a Trainium2 kernel written in Bass

```python
import numpy as np
import jax
import jax.numpy as jnp

def _softmax(x, axis=-1):
    return jax.nn.softmax(x, axis=axis)
def _gelu(x):
    return jax.nn.gelu(x, approximate=True)
def _silu(x):
    return jax.nn.silu(x)
def _sigmoid(x):
    return jax.nn.sigmoid(x)
def _layernorm(x, axis=-1, eps=1e-5):
    m = jnp.mean(x, axis=axis, keepdims=True)
    v = jnp.var(x, axis=axis, keepdims=True)
    return (x - m) / jnp.sqrt(v + eps)
def _scatter_add(tgt, idx, src, axis=0):
    return tgt.at[idx].add(src)
def _segment_sum(src, seg, n):
    return jax.ops.segment_sum(src, seg, n)

kernel_name = 'mk_conv_preact_d1_conv_nchw256_f5c960'

def setup_inputs(seed: int = 0):
    np.random.seed(seed)
    _w = jnp.asarray
    def _rec_inputs():
        import jax
        import jax.numpy as jnp
        _gk = jax.random.key(seed)
        x = -0.0003482 + 1 * jax.random.normal(jax.random.fold_in(_gk, 1), (8, 256, 96, 96), jnp.float32)
        return x
    x = _rec_inputs()
    def _L0_conv_setup():
        import jax, jax.numpy as jnp
        import numpy as np
        NUM_HEADS = 8
        DIM_HEAD_QK = 32
        DIM_HEAD_V = 32
        BLOCK = 8
        HALO = 3
        WIN = BLOCK + 2 * HALO
        SCALE = DIM_HEAD_QK ** (-0.5)

        def rel_logits_1d(q, rel_k, permute_mask):
            N, H, W, d = q.shape
            rel_size = rel_k.shape[0]
            win = (rel_size + 1) // 2
            x = jnp.einsum('nhwd,rd->nhwr', q, rel_k)
            x = x.reshape(N * H, W, rel_size)
            x = jnp.pad(x, ((0, 0), (0, 0), (0, 1))).reshape(N * H, -1)
            x = jnp.pad(x, ((0, 0), (0, rel_size - W)))
            x = x.reshape(N * H, W + 1, rel_size)[:, :W, win - 1:]
            x = jnp.broadcast_to(x.reshape(N, H, 1, W, win), (N, H, win, W, win))
            return jnp.transpose(x, permute_mask)

        def pos_embed_rel(q, height_rel, width_rel):
            BH, NB, HW, d = q.shape
            qb = q.reshape(-1, BLOCK, BLOCK, d)
            rel_w = rel_logits_1d(qb, width_rel, (0, 1, 3, 2, 4))
            rel_h = rel_logits_1d(jnp.swapaxes(qb, 1, 2), height_rel, (0, 3, 1, 4, 2))
            return (rel_h + rel_w).reshape(BH, NB, HW, WIN * WIN)
        key = jax.random.key(seed)
        k1, k2, k3, k4, k5 = jax.random.split(key, 5)
        dim = 256
        std = dim ** (-0.5)
        x = jax.random.normal(k1, (8, 256, 96, 96), dtype=jnp.float32)
        q_weight = jax.random.normal(k2, (256, 256), dtype=jnp.float32) * std
        kv_weight = jax.random.normal(k3, (512, 256), dtype=jnp.float32) * std
        height_rel = jax.random.normal(k4, (2 * WIN - 1, DIM_HEAD_QK), dtype=jnp.float32) * SCALE
        width_rel = jax.random.normal(k5, (2 * WIN - 1, DIM_HEAD_QK), dtype=jnp.float32) * SCALE
        return {'x': x, 'q_weight': q_weight, 'kv_weight': kv_weight, 'height_rel': height_rel, 'width_rel': width_rel}
    _L0_conv_all = _L0_conv_setup()
    _L0_conv_in = {k: v for k, v in _L0_conv_all.items() if k in ('q_weight', 'kv_weight', 'height_rel', 'width_rel', )}
    del _L0_conv_all

    return {
        "x": x,
        "L0_conv_q_weight": _L0_conv_in["q_weight"],
        "L0_conv_kv_weight": _L0_conv_in["kv_weight"],
        "L0_conv_height_rel": _L0_conv_in["height_rel"],
        "L0_conv_width_rel": _L0_conv_in["width_rel"],
    }

def reference(x, L0_conv_q_weight, L0_conv_kv_weight, L0_conv_height_rel, L0_conv_width_rel):
    import jax
    import jax.numpy as jnp
    def _L0_conv_ref(x, q_weight, kv_weight, height_rel, width_rel):
        import jax, jax.numpy as jnp
        import numpy as np
        NUM_HEADS = 8
        DIM_HEAD_QK = 32
        DIM_HEAD_V = 32
        BLOCK = 8
        HALO = 3
        WIN = BLOCK + 2 * HALO
        SCALE = DIM_HEAD_QK ** (-0.5)

        def rel_logits_1d(q, rel_k, permute_mask):
            N, H, W, d = q.shape
            rel_size = rel_k.shape[0]
            win = (rel_size + 1) // 2
            x = jnp.einsum('nhwd,rd->nhwr', q, rel_k)
            x = x.reshape(N * H, W, rel_size)
            x = jnp.pad(x, ((0, 0), (0, 0), (0, 1))).reshape(N * H, -1)
            x = jnp.pad(x, ((0, 0), (0, rel_size - W)))
            x = x.reshape(N * H, W + 1, rel_size)[:, :W, win - 1:]
            x = jnp.broadcast_to(x.reshape(N, H, 1, W, win), (N, H, win, W, win))
            return jnp.transpose(x, permute_mask)

        def pos_embed_rel(q, height_rel, width_rel):
            BH, NB, HW, d = q.shape
            qb = q.reshape(-1, BLOCK, BLOCK, d)
            rel_w = rel_logits_1d(qb, width_rel, (0, 1, 3, 2, 4))
            rel_h = rel_logits_1d(jnp.swapaxes(qb, 1, 2), height_rel, (0, 3, 1, 4, 2))
            return (rel_h + rel_w).reshape(BH, NB, HW, WIN * WIN)
        B, C, H, W = x.shape
        nhb, nwb = (H // BLOCK, W // BLOCK)
        nb = nhb * nwb
        q = jnp.einsum('bchw,oc->bohw', x, q_weight)
        q = q.reshape(B * NUM_HEADS, DIM_HEAD_QK, nhb, BLOCK, nwb, BLOCK)
        q = jnp.transpose(q, (0, 1, 3, 5, 2, 4)).reshape(B * NUM_HEADS, DIM_HEAD_QK, BLOCK * BLOCK, nb)
        q = jnp.swapaxes(q, 1, 3)
        kv = jnp.einsum('bchw,oc->bohw', x, kv_weight)
        kv = jnp.pad(kv, ((0, 0), (0, 0), (HALO, HALO), (HALO, HALO)))
        h_idx = jnp.arange(nhb)[:, None] * BLOCK + jnp.arange(WIN)[None, :]
        w_idx = jnp.arange(nwb)[:, None] * BLOCK + jnp.arange(WIN)[None, :]
        kv = kv[:, :, h_idx, :][:, :, :, :, w_idx]
        kv = jnp.transpose(kv, (0, 1, 2, 4, 3, 5)).reshape(B * NUM_HEADS, DIM_HEAD_QK + DIM_HEAD_V, nb, WIN * WIN)
        kv = jnp.transpose(kv, (0, 2, 3, 1))
        k, v = (kv[..., :DIM_HEAD_QK], kv[..., DIM_HEAD_QK:])
        attn = jnp.einsum('bnqd,bnkd->bnqk', q, k) * SCALE
        attn = attn + pos_embed_rel(q, height_rel, width_rel)
        attn = jax.nn.softmax(attn, axis=-1)
        out = jnp.einsum('bnqk,bnkd->bnqd', attn, v)
        out = jnp.swapaxes(out, 1, 3)
        out = out.reshape(-1, BLOCK, BLOCK, nhb, nwb)
        out = jnp.transpose(out, (0, 3, 1, 4, 2)).reshape(B, NUM_HEADS * DIM_HEAD_V, H, W)
        return out

    def _gn(v, G=32, eps=1e-5):
        B_, C_, H_, W_ = v.shape
        g = v.reshape(B_, G, C_ // G, H_, W_)
        m = jnp.mean(g, axis=(2, 3, 4), keepdims=True)
        s = jnp.var(g, axis=(2, 3, 4), keepdims=True)
        return ((g - m) / jnp.sqrt(s + eps)).reshape(v.shape)

    def _ln_c(v, eps=1e-6):
        m = jnp.mean(v, axis=1, keepdims=True)
        s = jnp.var(v, axis=1, keepdims=True)
        return (v - m) / jnp.sqrt(s + eps)

    def _ln_t(v, eps=1e-5):
        m = jnp.mean(v, axis=-1, keepdims=True)
        s = jnp.var(v, axis=-1, keepdims=True)
        return (v - m) / jnp.sqrt(s + eps)

    def _to_tokens(v):
        B_, C_, H_, W_ = v.shape
        return v.reshape(B_, C_, H_ * W_).transpose(0, 2, 1)
    def _from_tokens(t, like):
        B_, C_, H_, W_ = like.shape
        return t.transpose(0, 2, 1).reshape(B_, C_, H_, W_)

    x = x + _L0_conv_ref(_gn(x), L0_conv_q_weight, L0_conv_kv_weight, L0_conv_height_rel, L0_conv_width_rel)
    return x


_drawn_inputs = setup_inputs


def setup_inputs(seed=0):
    import zlib

    import numpy as np

    out = dict(_drawn_inputs(seed))
    spreads = {}
    factors = {}
    for name, (base, spread) in spreads.items():
        noise = np.random.default_rng([zlib.crc32(name.encode()), seed]).standard_normal(out[name].shape)
        drawn = base * np.exp(spread * noise) if base else spread * noise
        out[name] = jnp.asarray(drawn.astype(out[name].dtype))
    for name, factor in factors.items():
        out[name] = (out[name] * factor).astype(out[name].dtype)
    return out
```

```python
import numpy as np
import concourse.bass as bass
from concourse import mybir
from contextlib import ExitStack

F32 = mybir.dt.float32
F16 = mybir.dt.float16
ACT = mybir.ActivationFunctionType
ALU = mybir.AluOpType
AX = mybir.AxisListType

P = 128
IMGS, CH, SIDE = 8, 256, 96
HEADS, DH = 8, 32
BLOCK, HALO = 8, 3
WIN = BLOCK + 2 * HALO
KEYS = WIN * WIN
NQ = BLOCK * BLOCK
NB = SIDE // BLOCK
STRIPS = IMGS * NB
HALVES = CH // P
GROUPS = 2
PAIRS = 2
STEPS = GROUPS * NB
ROWS = 16
COLS = 104
VTILES = COLS // BLOCK
CHUNK = 6 * NQ
KCOLS = 32
TASKS = [("q", 0), ("k", 0), ("q", 1), ("k", 1), ("b", 0), ("k", 2), ("b", 1)]
NT = len(TASKS)
BATCH = 4
CLASSES = 2 * BLOCK
SCALE = float(DH) ** -0.5
EPS = 1e-5
TAB = 12


def build(nc, x, wq, wk, wv, relw, relh, onehot_c, ident_c, mean8_c, out):
    ctx = ExitStack()
    with ctx:
        def sb(name, shape, dt):
            return ctx.enter_context(nc.sbuf_tensor(name, shape, dt))

        def pb(name):
            return ctx.enter_context(nc.psum_tensor(name, [P, 512], F32))

        def sem(name):
            return ctx.enter_context(nc.semaphore(name))

        xraw = sb("xraw", [P, 2, HALVES, WIN * SIDE], F32)
        xs = sb("xs", [P, 2, 2, HALVES, COLS, ROWS], F16)
        xn = sb("xn", [P, WIN * SIDE], F32)
        kimg = sb("kimg", [P, GROUPS, 2, COLS, WIN], F16)
        qdiag = sb("qdiag", [P, GROUPS, 2, NB, PAIRS, 2 * NQ], F16)
        bdiag = sb("bdiag", [P, GROUPS, 2, NB, PAIRS, 2 * NQ], F16)
        vt = sb("vt", [P, 2, VTILES, CH], F16)
        qnat = sb("qnat", [P, 2, 2, CHUNK], F16)
        bnat = sb("bnat", [P, 2, 2, CHUNK], F16)
        prob = sb("prob", [P, 2, PAIRS, ROWS, ROWS], F32)
        pt = sb("pt", [P, 2, 2, 2, PAIRS, P], F16)
        negmax = sb("negmax", [P, 2, PAIRS], F32)
        sums = sb("sums", [P, 2, BATCH, PAIRS], F32)
        rinv = sb("rinv", [P, BATCH, PAIRS], F32)
        osb = sb("osb", [P, NB, GROUPS * PAIRS, DH], F32)
        ostage = sb("ostage", [P, HALVES, BLOCK, SIDE], F32)
        w_hl = sb("w_hl", [P, 3, 2, HALVES, CH], F16)
        r_hl = sb("r_hl", [P, 2, CLASSES, P], F16)
        onehot = sb("onehot", [P, KEYS], F16)
        ident = sb("ident", [P, P], F32)
        mean8 = sb("mean8", [P, P], F32)
        table = sb("table", [P, STRIPS + 2, TAB], F32)
        cur = sb("cur", [P, TAB], F32)
        bst = sb("bst", [P, HALVES, 2 * NB, 6], F32)
        mv = sb("mv", [P, HALVES, 2], F32)
        mvall = sb("mvall", [P, IMGS, HALVES, 2], F32)
        stat = sb("stat", [P, 6, IMGS * HALVES], F32)
        rraw = sb("rraw", [P, CLASSES, P], F32)
        wraw = vt[:, 0, :, :].rearrange("p m c -> p (m c)").bitcast(F32)[:, 0:3 * HALVES * CH]\
            .rearrange("p (w c) -> p w c", w=3)

        scores = [pb("scores0"), pb("scores1")]
        ptps = [pb("ptps0"), pb("ptps1")]
        ops = pb("ops")
        tps = pb("tps")
        vps = pb("vps")
        fps = pb("fps")

        const_in = sem("const_in")
        rel_zero = sem("rel_zero")
        zeros_set = sem("zeros_set")
        stat_in = [sem("stat_in0"), sem("stat_in1")]
        stat_used = sem("stat_used")
        w_scaled = sem("w_scaled")
        w_hi = sem("w_hi")
        w_lo = sem("w_lo")
        dve_step = sem("dve_step")
        pool_step = sem("pool_step")
        passed = sem("passed")
        moments = sem("moments")
        averaged = sem("averaged")
        rooted = sem("rooted")
        table_set = sem("table_set")
        x_in = [sem("x_in0"), sem("x_in1")]
        xs_ready = sem("xs_ready")
        task_done = sem("task_done")
        task_hi = sem("task_hi")
        task_lo = sem("task_lo")
        v_done = sem("v_done")
        v_hi = sem("v_hi")
        v_lo = sem("v_lo")
        s_done = sem("s_done")
        max_done = sem("max_done")
        exp_done = sem("exp_done")
        pt_done = sem("pt_done")
        pt_hi = sem("pt_hi")
        pt_lo = sem("pt_lo")
        pv_done = sem("pv_done")
        o_out = sem("o_out")
        fin_done = sem("fin_done")
        res_done = sem("res_done")
        out_sem = sem("out_sem")

        N_CONST = 16 * (6 + 8)
        block = ctx.enter_context(nc.Block())

        @block.sync
        def _(sp):
            for i, w in enumerate((wq, wk, wv)):
                sp.dma_start(wraw[:, i, :], w.rearrange("p h c -> p (h c)")).then_inc(const_in, 16)
            sp.dma_start(onehot[:], onehot_c).then_inc(const_in, 16)
            sp.dma_start(ident[:], ident_c).then_inc(const_in, 16)
            sp.dma_start(mean8[:], mean8_c).then_inc(const_in, 16)
            sp.wait_ge(rel_zero, 1)
            for h in range(4):
                dst = rraw[DH * h:DH * h + DH]
                sp.dma_start(dst[:, 0:BLOCK, DH * h + WIN:DH * h + 2 * WIN], relw).then_inc(const_in, 16)
                sp.dma_start(dst[:, BLOCK:CLASSES, DH * h:DH * h + WIN], relh).then_inc(const_in, 16)

            def load_rows(dst_par, b, n, row0, rows, done):
                sp.dma_start(xraw[:, dst_par, :, 0:rows * SIDE],
                             x[b, :, :, bass.ds(BLOCK * n + row0, rows), :]
                             .rearrange("p h r w -> p h (r w)")).then_inc(done, 16)

            with sp.Fori(0, IMGS) as b:
                for n in range(NB):
                    if n >= 2:
                        sp.wait_ge(stat_used, b * NB + (n - 1))
                    else:
                        sp.wait_ge(stat_used, b * NB)
                    load_rows(n % 2, b, n, HALO, BLOCK, stat_in[n % 2])
            sp.wait_ge(stat_used, STRIPS)
            for n in range(2):
                load_rows(n, 0, n, 0, WIN, x_in[n])
            with sp.Fori(0, IMGS - 1) as b:
                with sp.Fori(0, NB // 2 - 1) as n2:
                    for k in range(2):
                        sp.wait_ge(res_done, b * (3 * NB) + n2 * 6 + 3 * (k + 1))
                        load_rows(k, b, n2 * 2 + (k + 2), 0, WIN, x_in[k])
                for k in range(2):
                    sp.wait_ge(res_done, b * (3 * NB) + 3 * (NB - 2 + k + 1))
                    load_rows(k, b + 1, k, 0, WIN, x_in[k])
            with sp.Fori(0, NB // 2 - 1) as n2:
                for k in range(2):
                    sp.wait_ge(res_done, n2 * 6 + (3 * NB * (IMGS - 1) + 3 * (k + 1)))
                    load_rows(k, IMGS - 1, n2 * 2 + (k + 2), 0, WIN, x_in[k])
            for k in range(2):
                sp.wait_ge(res_done, 3 * (STRIPS - 2 + k + 1))
                load_rows(k, 0, k, 0, WIN, x_in[k])
            for k in range(2):
                sp.wait_ge(x_in[k], 16 * (STRIPS // 2 + 1))

        @block.gpsimd
        def _(pool):
            nc.gpsimd.memset(qdiag[:].rearrange("p g s m r q -> p (g s m r q)"), 0.0).then_inc(zeros_set, 1)
            nc.gpsimd.memset(bdiag[:].rearrange("p g s m r q -> p (g s m r q)"), 0.0).then_inc(zeros_set, 1)
            nc.gpsimd.memset(xs[:].rearrange("p k s h c r -> p (k s h c r)"), 0.0).then_inc(zeros_set, 1)
            nc.gpsimd.memset(kimg[:].rearrange("p g s c r -> p (g s c r)"), 0.0).then_inc(zeros_set, 1)
            nc.gpsimd.memset(prob[:].rearrange("p a b c r -> p (a b c r)"), 0.0).then_inc(zeros_set, 1)
            pool.wait_ge(zeros_set, 5)
            pool.wait_ge(table_set, 1)

            def normalise(par, t, loads):
                pool.wait_ge(x_in[par], loads)
                pool.sem_inc(passed, 1)
                pool.sem_clear(pool_step)
                nc.gpsimd.tensor_copy(cur[:].unsqueeze(1), table[:, bass.ds(t, 1), :]).then_inc(pool_step, 1)
                pool.wait_ge(pool_step, 1)
                done = 1
                for h in range(HALVES):
                    for kind, (r0, r1) in enumerate(((0, HALO), (HALO, HALO + BLOCK), (HALO + BLOCK, WIN))):
                        e = 4 * kind + 2 * h
                        nc.gpsimd.tensor_scalar(xn[:, r0 * SIDE:r1 * SIDE], xraw[:, par, h, r0 * SIDE:r1 * SIDE],
                                                cur[:, e:e + 1], cur[:, e + 1:e + 2], ALU.mult, ALU.add)\
                            .then_inc(pool_step, 1)
                        done += 1
                    pool.wait_ge(pool_step, done)
                    src = xn[:].rearrange("p (r c) -> p r c", c=SIDE)
                    hi = xs[:, par, 0, h, HALO:HALO + SIDE, 0:WIN].rearrange("p c r -> p r c")
                    lo = xs[:, par, 1, h, HALO:HALO + SIDE, 0:WIN].rearrange("p c r -> p r c")
                    nc.gpsimd.tensor_copy(hi, src).then_inc(pool_step, 1)
                    done += 1
                    pool.wait_ge(pool_step, done)
                    nc.gpsimd.tensor_tensor(lo, src, hi, ALU.subtract).then_inc(pool_step, 1)
                    done += 1
                    pool.wait_ge(pool_step, done)
                pool.sem_inc(xs_ready, 1)

            for k in range(2):
                normalise(k, k, 16)
            with pool.Fori(0, IMGS) as b:
                with pool.Fori(0, NB // 2) as n2:
                    for k in range(2):
                        t = pool.snap(b * NB + n2 * 2 + k)
                        pool.wait_ge(res_done, t * 3 + 3)
                        pool.dma_start(out[b, :, :, bass.ds(n2 * (2 * BLOCK) + BLOCK * k, BLOCK), :],
                                       ostage[:]).then_inc(out_sem, 16)
                        pool.wait_ge(task_done, t * (2 * NT) + 2 * NT)
                        normalise(k, t + 2, b * (8 * NB) + n2 * 16 + 32)
            pool.wait_ge(out_sem, 16 * STRIPS)

        def qview(par, hl, h, c):
            c0 = HALO + 48 * c
            return xs[:, par, hl, h, c0:c0 + 48, HALO:HALO + BLOCK]

        def kview(par, hl, h, c):
            c0 = HALO + KCOLS * c
            return xs[:, par, hl, h, c0:c0 + KCOLS, 0:WIN]

        PASSES = ((0, 0), (0, 1), (1, 0))

        @block.tensor
        def _(pe):
            pe.wait_ge(const_in, N_CONST)
            pe.wait_ge(moments, 1)
            nc.tensor.matmul(fps[:, 0:16], mean8[:], stat[:, 0, :], start=True, stop=True).then_inc(averaged, 1)
            pe.wait_ge(moments, 2)
            nc.tensor.matmul(fps[:, 16:32], mean8[:], stat[:, 1, :], start=True, stop=True).then_inc(averaged, 1)

            def task(k, g, par, idx):
                kind, c = TASKS[k]
                pe.wait_ge(task_lo, idx)
                if kind == "b":
                    first = True
                    for cls in range(CLASSES):
                        for ws, ms in PASSES:
                            src = qnat[:, c, ms, :]
                            dst = tps[:, 0:CHUNK]
                            if cls < BLOCK:
                                v, o = (a.rearrange("p (m j i) -> p m j i", i=BLOCK, j=BLOCK)[:, :, cls, :]
                                        for a in (src, dst))
                            else:
                                v, o = (a.rearrange("p (a i) -> p a i", i=BLOCK)[:, :, cls - BLOCK]
                                        for a in (src, dst))
                            mm = nc.tensor.matmul(o, r_hl[:, ws, cls, :], v, start=first,
                                                  stop=(cls == CLASSES - 1 and ws == 1), skip_group_check=True)
                            first = False
                else:
                    w = 0 if kind == "q" else 1
                    n = 0
                    for h in range(HALVES):
                        for ws, ms in PASSES:
                            if kind == "q":
                                v, cols = qview(par, ms, h, c), CHUNK
                            else:
                                v, cols = kview(par, ms, h, c), KCOLS * WIN
                            mm = nc.tensor.matmul(tps[:, 0:cols], w_hl[:, w, ws, h, P * g:P * g + P], v,
                                                  start=(n == 0), stop=(n == 5))
                            n += 1
                mm.then_inc(task_done, 1)

            def values(m, par, idx):
                pe.wait_ge(v_lo, idx)
                n = 0
                for h in range(HALVES):
                    for ws, ms in PASSES:
                        tile = xs[:, par, ws, h, BLOCK * m:BLOCK * m + BLOCK, :].rearrange("p c r -> p (c r)")
                        mm = nc.tensor.matmul(vps[:, 0:CH], tile, w_hl[:, 2, ms, h, :],
                                              start=(n == 0), stop=(n == 5))
                        n += 1
                mm.then_inc(v_done, 1)

            def score(s, q, half):
                g, m, buf = s // NB, s % NB, s % 2
                if q is not None:
                    pe.wait_ge(exp_done, q - 1)
                if m == 0:
                    pe.wait_ge(task_lo, half)
                for r in range(PAIRS):
                    o = scores[buf][:, KEYS * r:KEYS * r + KEYS]
                    for n, (ws, ms) in enumerate(PASSES):
                        nc.tensor.matmul(o, qdiag[:, g, ws, m, r, :],
                                         kimg[:, g, ms, BLOCK * m:BLOCK * m + WIN, :],
                                         start=(n == 0), stop=False)
                    for ws in range(2):
                        mm = nc.tensor.matmul(o, bdiag[:, g, ws, m, r, :], onehot[:],
                                              start=False, stop=(ws == 1))
                mm.then_inc(s_done, 1)

            def turn(s, q):
                buf = s % 2
                pe.wait_ge(exp_done, q + 1)
                if not isinstance(q, int) or q >= 2:
                    pe.wait_ge(pt_lo, q - 1)
                for tile in range(2):
                    for r in range(PAIRS):
                        c = (tile * PAIRS + r) * P
                        keys = prob[:, buf, r, BLOCK * tile:BLOCK * tile + BLOCK, :].rearrange("p c r -> p (c r)")
                        mm = nc.tensor.transpose(ptps[buf][:, c:c + P], keys, ident[:])
                mm.then_inc(pt_done, 1)

            def weigh(s, q, vcount):
                g, m, buf = s // NB, s % NB, s % 2
                pe.wait_ge(pt_lo, q + 1)
                if g == 0:
                    pe.wait_ge(v_lo, vcount)
                if m % BATCH == 0:
                    pe.wait_ge(o_out, q_batches(q, s))
                for r in range(PAIRS):
                    o = ops[:, (m % BATCH * PAIRS + r) * 64:(m % BATCH * PAIRS + r) * 64 + 64]
                    c = 64 * (PAIRS * g + r)
                    n = 0
                    for tile in range(2):
                        for ws, ms in PASSES:
                            mm = nc.tensor.matmul(o, pt[:, buf, ws, tile, r, :],
                                                  vt[:, ms, m + tile, c:c + 64],
                                                  start=(n == 0), stop=(n == 5))
                            n += 1
                mm.then_inc(pv_done, 1)

            def finish(bt, batches, fins):
                pe.wait_ge(o_out, batches)
                pe.wait_ge(res_done, fins)
                for j in range(BATCH):
                    m = BATCH * bt + j
                    mm = nc.tensor.transpose(fps[:, P * j:P * j + P],
                                             osb[:, m, :, :].rearrange("p r d -> p (r d)"), ident[:])
                mm.then_inc(fin_done, 1)

            strip = {}

            def q_batches(q, s):
                return strip["batches"] + s // BATCH

            pe.wait_ge(zeros_set, 5)
            pe.wait_ge(w_lo, 2)
            pe.wait_ge(xs_ready, 1)
            for k in range(NT):
                task(k, 0, 0, k)
            for m in range(VTILES):
                values(m, 0, m)
            score(0, None, NT)
            score(1, None, NT)
            turn(0, 0)
            with pe.Fori(0, STRIPS // 2) as t2:
                q0 = pe.snap(t2 * (2 * STEPS))
                k0 = pe.snap(t2 * (4 * NT) + NT)
                v0 = pe.snap(t2 * (2 * VTILES) + VTILES)
                b0 = pe.snap(t2 * 12)
                f0 = pe.snap(t2 * 6)
                x0 = pe.snap(t2 * 2)
                for k in range(2):
                    strip["batches"] = b0 + 6 * k
                    for s in range(STEPS):
                        q = q0 + (STEPS * k + s)
                        s2 = (s + 2) % STEPS
                        score(s2, q + 2, k0 + (2 * NT * k + (NT if s2 == NB else 2 * NT)))
                        turn((s + 1) % STEPS, q + 1)
                        if s == NB:
                            pe.wait_ge(xs_ready, x0 + (k + 2))
                        if s % NB < NT:
                            if s < NB:
                                task(s, 1, k, k0 + (2 * NT * k + s))
                            else:
                                task(s - NB, 0, 1 - k, k0 + (2 * NT * k + NT + s - NB))
                        weigh(s, q, v0 + (VTILES * (k - 1) + s + 2))
                        if s >= NB:
                            values(s - NB, 1 - k, v0 + (VTILES * k + s - NB))
                        if s == STEPS - 1:
                            values(NB, 1 - k, v0 + (VTILES * k + NB))
                        if s in (16, 20):
                            bt = (s - 16) // 4
                            finish(bt, b0 + (6 * k + 4 + bt), f0 + (3 * k + bt))
                    finish(2, b0 + (6 * k + 6), f0 + (3 * k + 2))

        @block.scalar
        def _(act):
            act.wait_ge(w_scaled, 1)
            nc.scalar.activation(w_hl[:, :, 0, :, :].rearrange("p w h c -> p w (h c)"), wraw, ACT.Copy)\
                .then_inc(w_hi, 1)
            nc.scalar.activation(r_hl[:, 0, :, :], rraw[:], ACT.Copy).then_inc(w_hi, 1)

            act.wait_ge(moments, 3)
            nc.scalar.activation(stat[:, 5, :], stat[:, 4, :], ACT.Sqrt).then_inc(rooted, 1)

            def task(k, g, idx):
                kind, c = TASKS[k]
                act.wait_ge(task_done, idx + 1)
                if kind == "k":
                    c0 = HALO + KCOLS * c
                    nc.scalar.activation(kimg[:, g, 0, c0:c0 + KCOLS, :],
                                         tps[:, 0:KCOLS * WIN].rearrange("p (c r) -> p c r", r=WIN),
                                         ACT.Copy).then_inc(task_hi, 1)
                else:
                    dst = qnat if kind == "q" else bnat
                    nc.scalar.activation(dst[:, c, 0, :], tps[:, 0:CHUNK], ACT.Copy).then_inc(task_hi, 1)

            def values(m, idx):
                act.wait_ge(v_done, idx + 1)
                nc.scalar.activation(vt[:, 0, m, :], vps[:, 0:CH], ACT.Copy).then_inc(v_hi, 1)

            def expo(s, q, batches):
                buf, m = s % 2, s % NB
                act.wait_ge(max_done, q + 1)
                if not isinstance(q, int):
                    act.wait_ge(pt_done, q - 1)
                if batches is not None:
                    act.wait_ge(o_out, batches)
                for r in range(PAIRS):
                    e = nc.scalar.activation(prob[:, buf, r, 0:WIN, 0:WIN],
                                             scores[buf][:, KEYS * r:KEYS * r + KEYS]
                                             .rearrange("p (c r) -> p c r", r=WIN), ACT.Exp, bias=negmax[:, buf, r:r + 1],
                                             accum_out=sums[:, (s // BATCH) % 2, m % BATCH, r:r + 1])
                e.then_inc(exp_done, 1)

            def high(s, q):
                buf = s % 2
                act.wait_ge(pt_done, q + 1)
                if not isinstance(q, int):
                    act.wait_ge(pv_done, q - 1)
                nc.scalar.activation(pt[:, buf, 0, :, :, :].rearrange("p t r c -> p (t r c)"),
                                     ptps[buf][:, :], ACT.Copy).then_inc(pt_hi, 1)

            act.wait_ge(zeros_set, 5)
            act.wait_ge(w_lo, 2)
            for k in range(NT):
                task(k, 0, k)
            for m in range(VTILES):
                values(m, m)
            expo(0, 0, None)
            expo(1, 1, None)
            high(0, 0)
            with act.Fori(0, STRIPS // 2) as t2:
                q0 = act.snap(t2 * (2 * STEPS))
                k0 = act.snap(t2 * (4 * NT) + NT)
                v0 = act.snap(t2 * (2 * VTILES) + VTILES)
                b0 = act.snap(t2 * 12)
                for k in range(2):
                    for s in range(STEPS):
                        q = q0 + (STEPS * k + s)
                        new = (s + 2) % BATCH == 0
                        expo((s + 2) % STEPS, q + 2, b0 + (6 * k + (s + 2) // BATCH - 1) if new else None)
                        high((s + 1) % STEPS, q + 1)
                        if s % NB < NT:
                            if s < NB:
                                task(s, 1, k0 + (2 * NT * k + s))
                            else:
                                task(s - NB, 0, k0 + (2 * NT * k + NT + s - NB))
                        if s >= NB:
                            values(s - NB, v0 + (VTILES * k + s - NB))
                        if s == STEPS - 1:
                            values(NB, v0 + (VTILES * k + NB))

        @block.vector
        def _(dve):
            own = [0]

            def settle(ins):
                own[0] += 1
                ins.then_inc(dve_step, 1)
                dve.wait_ge(dve_step, own[0])

            nc.vector.memset(rraw[:], 0.0).then_inc(rel_zero, 1)
            dve.wait_ge(const_in, N_CONST)
            dve.wait_ge(rel_zero, 1)
            nc.vector.tensor_scalar(wraw[:, 1, :], wraw[:, 1, :], SCALE, None, ALU.mult).then_inc(w_scaled, 1)
            dve.wait_ge(w_scaled, 1)
            dve.wait_ge(w_hi, 1)
            nc.vector.tensor_tensor(w_hl[:, :, 1, :, :].rearrange("p w h c -> p w (h c)"), wraw,
                                    w_hl[:, :, 0, :, :].rearrange("p w h c -> p w (h c)"), ALU.subtract)\
                .then_inc(w_lo, 1)
            dve.wait_ge(w_hi, 2)
            nc.vector.tensor_tensor(r_hl[:, 1, :, :], rraw[:], r_hl[:, 0, :, :], ALU.subtract).then_inc(w_lo, 1)

            half = BLOCK * SIDE // 2
            with dve.Fori(0, IMGS) as b:
                for n in range(NB):
                    dve.wait_ge(stat_in[n % 2], b * (8 * NB) + 16 * (n // 2 + 1))
                    for h in range(HALVES):
                        for c in range(2):
                            st = nc.vector.bn_stats(bst[:, h, 2 * n + c, :],
                                                    xraw[:, n % 2, h, half * c:half * c + half])
                    st.then_inc(stat_used, 1)
                dve.wait_ge(stat_used, b * NB + NB)
                dve.sem_inc(passed, 1)
                for h in range(HALVES):
                    st = nc.vector.bn_aggr(mv[:, h, :], bst[:, h, :, :])
                st.then_inc(dve_step, 1)
                dve.wait_ge(dve_step, b * 2 + 1)
                nc.vector.tensor_copy(mvall[:, bass.ds(b, 1), :, :], mv[:].unsqueeze(1)).then_inc(dve_step, 1)
                dve.wait_ge(dve_step, b * 2 + 2)
            own[0] = 2 * IMGS
            means = mvall[:].rearrange("p b h s -> p (b h) s")[:, :, 0]
            varis = mvall[:].rearrange("p b h s -> p (b h) s")[:, :, 1]
            nc.vector.tensor_copy(stat[:, 0, :], means).then_inc(moments, 1)
            dve.wait_ge(averaged, 1)
            settle(nc.vector.tensor_copy(stat[:, 2, :], fps[:, 0:16]))
            settle(nc.vector.tensor_tensor(stat[:, 3, :], means, stat[:, 2, :], ALU.subtract))
            settle(nc.vector.tensor_tensor(stat[:, 3, :], stat[:, 3, :], stat[:, 3, :], ALU.mult))
            nc.vector.tensor_tensor(stat[:, 1, :], varis, stat[:, 3, :], ALU.add).then_inc(moments, 1)
            dve.wait_ge(averaged, 2)
            nc.vector.tensor_scalar(stat[:, 4, :], fps[:, 16:32], EPS, None, ALU.add).then_inc(moments, 1)
            dve.wait_ge(rooted, 1)
            settle(nc.vector.reciprocal(stat[:, 3, :], stat[:, 5, :]))
            settle(nc.vector.tensor_tensor(stat[:, 5, :], stat[:, 3, :], stat[:, 3, :], ALU.mult))
            settle(nc.vector.tensor_tensor(stat[:, 5, :], stat[:, 5, :], stat[:, 4, :], ALU.mult))
            settle(nc.vector.tensor_scalar(stat[:, 5, :], stat[:, 5, :], -0.5, 1.5, ALU.mult, ALU.add))
            settle(nc.vector.tensor_tensor(stat[:, 3, :], stat[:, 3, :], stat[:, 5, :], ALU.mult))
            settle(nc.vector.scalar_tensor_tensor(out=stat[:, 1, :], in0=stat[:, 2, :], scalar=-1.0,
                                                  in1=stat[:, 3, :], op0=ALU.mult, op1=ALU.mult))
            settle(nc.vector.memset(table[:].rearrange("p t e -> p (t e)"), 0.0))
            for b in range(IMGS):
                for e in range(2):
                    src = stat[:, 3 if e == 0 else 1, 2 * b:2 * b + 2]
                    for kind in range(3):
                        dst = table[:, NB * b:NB * b + NB, 4 * kind + e:4 * kind + e + 3:2]
                        first, last = (1 if kind == 0 else 0), (NB - 1 if kind == 2 else NB)
                        settle(nc.vector.tensor_copy(dst[:, first:last, :],
                                                     src.unsqueeze(1).to_broadcast([P, last - first, 2])))
            nc.vector.memset(negmax[:].rearrange("p a b -> p (a b)"), 0.0).then_inc(table_set, 1)
            dve.wait_ge(zeros_set, 5)
            step0 = own[0]
            
            def lo_of(dst, src, hi):
                return nc.vector.tensor_tensor(dst, src, hi, ALU.subtract)

            def task(k, g, idx, steps):
                kind, c = TASKS[k]
                dve.wait_ge(task_hi, idx + 1)
                if kind == "k":
                    c0 = HALO + KCOLS * c
                    lo_of(kimg[:, g, 1, c0:c0 + KCOLS, :],
                          tps[:, 0:KCOLS * WIN].rearrange("p (c r) -> p c r", r=WIN),
                          kimg[:, g, 0, c0:c0 + KCOLS, :]).then_inc(task_lo, 1)
                    return steps
                nat, diag = (qnat, qdiag) if kind == "q" else (bnat, bdiag)
                lo_of(nat[:, c, 1, :], tps[:, 0:CHUNK], nat[:, c, 0, :]).then_inc(dve_step, 1)
                dve.wait_ge(dve_step, steps + 1)
                for h in range(4):
                    p0 = DH * h
                    ins = nc.vector.tensor_copy(
                        diag[p0:p0 + DH, g, :, 6 * c:6 * c + 6, h // 2, NQ * (h % 2):NQ * (h % 2) + NQ],
                        nat[p0:p0 + DH, c, :, :].rearrange("p s (m q) -> p s m q", q=NQ))
                ins.then_inc(task_lo, 1)
                return steps + 1

            def values(m, idx):
                dve.wait_ge(v_hi, idx + 1)
                lo_of(vt[:, 1, m, :], vps[:, 0:CH], vt[:, 0, m, :]).then_inc(v_lo, 1)

            def maxima(s, q):
                buf = s % 2
                dve.wait_ge(s_done, q + 1)
                nc.vector.tensor_reduce(negmax[:, buf, :],
                                        scores[buf][:, 0:PAIRS * KEYS].rearrange("p (r k) -> p r k", r=PAIRS),
                                        axis=AX.X, op=ALU.max, negate=True).then_inc(max_done, 1)

            def low(s, q):
                buf = s % 2
                dve.wait_ge(pt_hi, q + 1)
                lo_of(pt[:, buf, 1, :, :, :].rearrange("p t r c -> p (t r c)"), ptps[buf][:, :],
                      pt[:, buf, 0, :, :, :].rearrange("p t r c -> p (t r c)")).then_inc(pt_lo, 1)

            def outputs(s, q, steps):
                g, bt = s // NB, (s % NB) // BATCH
                dve.wait_ge(pv_done, q + 1)
                nc.vector.reciprocal(rinv[:], sums[:, (s // BATCH) % 2, :, :]).then_inc(dve_step, 1)
                dve.wait_ge(dve_step, steps + 1)
                for half_ in range(2):
                    p0 = NQ * half_
                    src = ops[p0:p0 + NQ, :].rearrange("p (m r c) -> p m r c", m=BATCH, r=PAIRS)[
                        :, :, :, DH * half_:DH * half_ + DH]
                    ins = nc.vector.tensor_tensor(
                        osb[p0:p0 + NQ, BATCH * bt:BATCH * bt + BATCH, PAIRS * g:PAIRS * g + PAIRS, :], src,
                        rinv[p0:p0 + NQ, :, :].unsqueeze(3).to_broadcast([NQ, BATCH, PAIRS, DH]), ALU.mult)
                ins.then_inc(o_out, 1)
                return steps + 1

            def residual(bt, par, idx, stored):
                dve.wait_ge(fin_done, idx + 1)
                if stored is not None:
                    dve.wait_ge(out_sem, stored)
                c0 = BATCH * bt * BLOCK
                for h in range(HALVES):
                    src = fps[:].rearrange("p (m h j i) -> p h i m j", m=BATCH, h=HALVES, j=BLOCK)[:, h]
                    xr = xraw[:, par, h, HALO * SIDE:(HALO + BLOCK) * SIDE]\
                        .rearrange("p (i c) -> p i c", c=SIDE)[:, :, c0:c0 + BATCH * BLOCK]\
                        .rearrange("p i (m j) -> p i m j", j=BLOCK)
                    dst = ostage[:, h, :, c0:c0 + BATCH * BLOCK].rearrange("p i (m j) -> p i m j", j=BLOCK)
                    ins = nc.vector.tensor_tensor(dst, src, xr, ALU.add)
                ins.then_inc(res_done, 1)

            st = step0
            for k in range(NT):
                st = task(k, 0, k, st)
            for m in range(VTILES):
                values(m, m)
            maxima(0, 0)
            maxima(1, 1)
            low(0, 0)
            per = 8 + 6
            with dve.Fori(0, STRIPS // 2) as t2:
                q0 = dve.snap(t2 * (2 * STEPS))
                k0 = dve.snap(t2 * (4 * NT) + NT)
                v0 = dve.snap(t2 * (2 * VTILES) + VTILES)
                d0 = dve.snap(t2 * (2 * per))
                f0 = dve.snap(t2 * 6)
                o0 = dve.snap(t2 * 32)
                for k in range(2):
                    n = st + per * k
                    for s in range(STEPS):
                        q = q0 + (STEPS * k + s)
                        maxima((s + 2) % STEPS, q + 2)
                        low((s + 1) % STEPS, q + 1)
                        if s % NB < NT:
                            kk = s % NB
                            idx = k0 + (2 * NT * k + (kk if s < NB else NT + kk))
                            task(kk, 1 if s < NB else 0, idx, d0 + n)
                            n += TASKS[kk][0] != "k"
                        if s % BATCH == BATCH - 1:
                            outputs(s, q, d0 + n)
                            n += 1
                        if s >= NB:
                            values(s - NB, v0 + (VTILES * k + s - NB))
                        if s == STEPS - 1:
                            values(NB, v0 + (VTILES * k + NB))
                        if s in (16, 20):
                            bt = (s - 16) // 4
                            residual(bt, k, f0 + (3 * k + bt), o0 + 16 * k if bt == 0 else None)
                    residual(2, k, f0 + (3 * k + 2), None)
                    assert n == st + per * (k + 1)


def kernel(x, L0_conv_q_weight, L0_conv_kv_weight, L0_conv_height_rel, L0_conv_width_rel):
    import concourse.bacc as bacc
    from concourse.bass_utils import run_bass_kernel_spmd as run

    x = np.asarray(x)
    q_w, kv_w = np.asarray(L0_conv_q_weight), np.asarray(L0_conv_kv_weight)
    h_rel, w_rel = np.asarray(L0_conv_height_rel), np.asarray(L0_conv_width_rel)

    xp = np.zeros((IMGS, P, HALVES, SIDE + 2 * HALO, SIDE), np.float32)
    xp[:, :, :, HALO:HALO + SIDE] = x.reshape(IMGS, 4, 2, DH, SIDE, SIDE).transpose(0, 1, 3, 2, 4, 5)\
        .reshape(IMGS, P, HALVES, SIDE, SIDE)

    def lay(w):
        return np.ascontiguousarray(w.reshape(CH, 4, 2, DH).transpose(1, 3, 2, 0).reshape(P, HALVES, CH))

    kv = kv_w.reshape(HEADS, 2, DH, CH)
    windows = np.arange(WIN)[None, :] + (WIN - 1) - np.arange(BLOCK)[:, None]
    arrays = {
        "x": xp,
        "wq": lay(q_w),
        "wk": lay(kv[:, 0].reshape(CH, CH)),
        "wv": lay(kv[:, 1].reshape(CH, CH)),
        "relw": np.ascontiguousarray(w_rel[windows].transpose(2, 0, 1)),
        "relh": np.ascontiguousarray(h_rel[windows].transpose(2, 0, 1)),
    }
    oh = np.zeros((4, DH, WIN, WIN), np.float16)
    for a in range(WIN):
        oh[:, a, :, a] = 1
        oh[:, WIN + a, a, :] = 1
    arrays["onehot"] = oh.reshape(P, KEYS)
    arrays["ident"] = np.eye(P, dtype=np.float32)
    arrays["mean8"] = np.kron(np.eye(P // 8), np.full((8, 8), 1 / 8)).astype(np.float32)

    nc = bacc.Bacc("TRN2", target_bir_lowering=False, num_devices=1)
    args = [nc.dram_tensor("in_" + n, a.shape, mybir.dt.from_np(a.dtype), kind="ExternalInput").ap()
            for n, a in arrays.items()]
    out = nc.dram_tensor("out_x", (IMGS, P, HALVES, SIDE, SIDE), F32, kind="ExternalOutput").ap()
    build(nc, *args, out)
    r = run(nc, [{"in_" + n: a for n, a in arrays.items()}], core_ids=[0])
    got = r.results[0]["out_x"]
    return np.ascontiguousarray(got.reshape(IMGS, 4, DH, 2, SIDE, SIDE).transpose(0, 1, 3, 2, 4, 5)
                                .reshape(IMGS, CH, SIDE, SIDE))
```

```python
import numpy as np
import concourse.bass as bass
from concourse import mybir
from contextlib import ExitStack

F32 = mybir.dt.float32
F16 = mybir.dt.float16
ACT = mybir.ActivationFunctionType
ALU = mybir.AluOpType
AX = mybir.AxisListType

P = 128
IMGS, CH, SIDE = 8, 256, 96
HEADS, DH = 8, 32
BLOCK, HALO = 8, 3
WIN = BLOCK + 2 * HALO
KEYS = WIN * WIN
NQ = BLOCK * BLOCK
NB = SIDE // BLOCK
STRIPS = IMGS * NB
HALVES = CH // P
GROUPS = 2
PAIRS = 2
STEPS = GROUPS * NB
ROWS = 16
COLS = 104
VTILES = COLS // BLOCK
CHUNK = 6 * NQ
KCOLS = 32
TASKS = [("q", 0), ("k", 0), ("q", 1), ("k", 1), ("b", 0), ("k", 2), ("b", 1)]
NT = len(TASKS)


def projections():
    plan = [[] for _ in range(STEPS)]
    for k in range(NT):
        plan[k].append(("t", k))
        plan[NB + k].append(("t", k))
    free = list(range(NB, NB + 10)) + [NB + NT, NB + NT + 1, NB + NT + 2]
    for v, step in enumerate(sorted(free)):
        plan[step].append(("v", v))
    return plan


BATCH = 4
CLASSES = 2 * BLOCK
SCALE = float(DH) ** -0.5
EPS = 1e-5
PLAN = projections()
PROJ = sum(map(len, PLAN))
AHEAD = NT + VTILES
VX_STEP = NB
assert PROJ == 2 * NT + VTILES
TAB = 12


def build(nc, x, wq, wk, wv, relw, relh, onehot_c, ident_c, mean8_c, out):
    ctx = ExitStack()
    with ctx:
        def sb(name, shape, dt):
            return ctx.enter_context(nc.sbuf_tensor(name, shape, dt))

        def pb(name):
            return ctx.enter_context(nc.psum_tensor(name, [P, 512], F32))

        def sem(name):
            return ctx.enter_context(nc.semaphore(name))

        xraw = sb("xraw", [P, 2, HALVES, WIN * SIDE], F32)
        xs = sb("xs", [P, 2, 2, HALVES, COLS, ROWS], F16)
        xn = sb("xn", [P, WIN * SIDE], F32)
        kimg = sb("kimg", [P, GROUPS, 2, COLS, WIN], F16)
        qdiag = sb("qdiag", [P, GROUPS, 2, NB, PAIRS, 2 * NQ], F16)
        bdiag = sb("bdiag", [P, GROUPS, 2, NB, PAIRS, 2 * NQ], F16)
        vt = sb("vt", [P, 2, 2, VTILES, CH], F16)
        qnat = sb("qnat", [P, 2, 2, CHUNK], F16)
        bnat = sb("bnat", [P, 2, 2, CHUNK], F16)
        prob = sb("prob", [P, 2, PAIRS, ROWS, ROWS], F32)
        pt = sb("pt", [P, 2, 2, 2, PAIRS, P], F16)
        negmax = sb("negmax", [P, 2, PAIRS], F32)
        sums = sb("sums", [P, 2, BATCH, PAIRS], F32)
        rinv = sb("rinv", [P, BATCH, PAIRS], F32)
        osb = sb("osb", [P, NB, GROUPS * PAIRS, DH], F32)
        ostage = sb("ostage", [P, HALVES, BLOCK, SIDE], F32)
        w_hl = sb("w_hl", [P, 3, 2, HALVES, CH], F16)
        r_hl = sb("r_hl", [P, 2, CLASSES, P], F16)
        onehot = sb("onehot", [P, KEYS], F16)
        ident = sb("ident", [P, P], F32)
        mean8 = sb("mean8", [P, P], F32)
        table = sb("table", [P, STRIPS + 2, TAB], F32)
        cur = sb("cur", [P, TAB], F32)
        bst = sb("bst", [P, HALVES, 2 * NB, 6], F32)
        mv = sb("mv", [P, HALVES, 2], F32)
        mvall = sb("mvall", [P, IMGS, HALVES, 2], F32)
        stat = sb("stat", [P, 6, IMGS * HALVES], F32)
        wraw, rraw = (vt[:, k].rearrange("p s m c -> p (s m c)").bitcast(F32)[:, 0:n]
                      for k, n in enumerate((3 * HALVES * CH, CLASSES * P)))
        wraw = wraw.rearrange("p (w c) -> p w c", w=3)
        rraw = rraw.rearrange("p (k c) -> p k c", k=CLASSES)

        scores = [pb("scores0"), pb("scores1")]
        ptps = [pb("ptps0"), pb("ptps1")]
        ops = pb("ops")
        proj = [pb("proj0"), pb("proj1")]
        fps = pb("fps")

        const_in = sem("const_in")
        rel_zero = sem("rel_zero")
        zeros_set = sem("zeros_set")
        stat_in = [sem("stat_in0"), sem("stat_in1")]
        stat_used = sem("stat_used")
        w_scaled = sem("w_scaled")
        w_hi = sem("w_hi")
        w_lo = sem("w_lo")
        dve_step = sem("dve_step")
        pool_step = sem("pool_step")
        passed = sem("passed")
        moments = sem("moments")
        averaged = sem("averaged")
        rooted = sem("rooted")
        table_set = sem("table_set")
        x_in = [sem("x_in0"), sem("x_in1")]
        xs_ready = sem("xs_ready")
        proj_done = sem("proj_done")
        proj_hi = sem("proj_hi")
        proj_lo = sem("proj_lo")
        s_done = sem("s_done")
        max_done = sem("max_done")
        exp_done = sem("exp_done")
        pt_done = sem("pt_done")
        pt_hi = sem("pt_hi")
        pt_lo = sem("pt_lo")
        pv_done = sem("pv_done")
        o_out = sem("o_out")
        fin_done = sem("fin_done")
        res_done = sem("res_done")
        out_sem = sem("out_sem")
        stage_free = sem("stage_free")

        N_CONST = 16 * (6 + 8)
        HEAD = 1
        block = ctx.enter_context(nc.Block())

        @block.sync
        def _(sp):
            for i, w in enumerate((wq, wk, wv)):
                sp.dma_start(wraw[:, i, :], w.rearrange("p h c -> p (h c)")).then_inc(const_in, 16)
            sp.dma_start(onehot[:], onehot_c).then_inc(const_in, 16)
            sp.dma_start(ident[:], ident_c).then_inc(const_in, 16)
            sp.dma_start(mean8[:], mean8_c).then_inc(const_in, 16)
            sp.wait_ge(rel_zero, 1)
            for h in range(4):
                dst = rraw[DH * h:DH * h + DH]
                sp.dma_start(dst[:, 0:BLOCK, DH * h + WIN:DH * h + 2 * WIN], relw).then_inc(const_in, 16)
                sp.dma_start(dst[:, BLOCK:CLASSES, DH * h:DH * h + WIN], relh).then_inc(const_in, 16)

            def load_rows(dst_par, b, n, row0, rows, done):
                sp.dma_start(xraw[:, dst_par, :, 0:rows * SIDE],
                             x[b, :, :, bass.ds(BLOCK * n + row0, rows), :]
                             .rearrange("p h r w -> p h (r w)")).then_inc(done, 16)

            with sp.Fori(0, IMGS) as b:
                for n in range(NB):
                    if n >= 2:
                        sp.wait_ge(stat_used, b * NB + (n - 1 + HEAD))
                    else:
                        sp.wait_ge(stat_used, b * NB + HEAD)
                    load_rows(n % 2, b, n, HALO, BLOCK, stat_in[n % 2])
            sp.wait_ge(stat_used, STRIPS + HEAD)
            for n in range(2):
                load_rows(n, 0, n, 0, WIN, x_in[n])
            with sp.Fori(0, IMGS - 1) as b:
                with sp.Fori(0, NB // 2 - 1) as n2:
                    for k in range(2):
                        sp.wait_ge(res_done, b * (3 * NB) + n2 * 6 + (3 * (k + 1) + HEAD))
                        load_rows(k, b, n2 * 2 + (k + 2), 0, WIN, x_in[k])
                for k in range(2):
                    sp.wait_ge(res_done, b * (3 * NB) + (3 * (NB - 2 + k + 1) + HEAD))
                    load_rows(k, b + 1, k, 0, WIN, x_in[k])
            with sp.Fori(0, NB // 2 - 1) as n2:
                for k in range(2):
                    sp.wait_ge(res_done, n2 * 6 + (3 * NB * (IMGS - 1) + 3 * (k + 1) + HEAD))
                    load_rows(k, IMGS - 1, n2 * 2 + (k + 2), 0, WIN, x_in[k])
            for k in range(2):
                sp.wait_ge(res_done, 3 * (STRIPS - 2 + k + 1) + HEAD)
                load_rows(k, 0, k, 0, WIN, x_in[k])
            for k in range(2):
                sp.wait_ge(x_in[k], 16 * (STRIPS // 2 + 1))

        @block.gpsimd
        def _(pool):
            nc.gpsimd.memset(qdiag[:].rearrange("p g s m r q -> p (g s m r q)"), 0.0).then_inc(zeros_set, 1)
            nc.gpsimd.memset(bdiag[:].rearrange("p g s m r q -> p (g s m r q)"), 0.0).then_inc(zeros_set, 1)
            nc.gpsimd.memset(xs[:].rearrange("p k s h c r -> p (k s h c r)"), 0.0).then_inc(zeros_set, 1)
            nc.gpsimd.memset(kimg[:].rearrange("p g s c r -> p (g s c r)"), 0.0).then_inc(zeros_set, 1)
            nc.gpsimd.memset(prob[:].rearrange("p a b c r -> p (a b c r)"), 0.0).then_inc(zeros_set, 1)
            pool.sem_inc(stage_free, HEAD)
            pool.wait_ge(zeros_set, 5)
            pool.wait_ge(table_set, 1)

            def normalise(par, t, loads):
                pool.wait_ge(x_in[par], loads)
                pool.sem_inc(passed, 1)
                pool.sem_clear(pool_step)
                nc.gpsimd.tensor_copy(cur[:].unsqueeze(1), table[:, bass.ds(t, 1), :]).then_inc(pool_step, 1)
                pool.wait_ge(pool_step, 1)
                done = 1
                for h in range(HALVES):
                    for kind, (r0, r1) in enumerate(((0, HALO), (HALO, HALO + BLOCK), (HALO + BLOCK, WIN))):
                        e = 4 * kind + 2 * h
                        nc.gpsimd.tensor_scalar(xn[:, r0 * SIDE:r1 * SIDE], xraw[:, par, h, r0 * SIDE:r1 * SIDE],
                                                cur[:, e:e + 1], cur[:, e + 1:e + 2], ALU.mult, ALU.add)\
                            .then_inc(pool_step, 1)
                        done += 1
                    pool.wait_ge(pool_step, done)
                    src = xn[:].rearrange("p (r c) -> p r c", c=SIDE)
                    hi = xs[:, par, 0, h, HALO:HALO + SIDE, 0:WIN].rearrange("p c r -> p r c")
                    lo = xs[:, par, 1, h, HALO:HALO + SIDE, 0:WIN].rearrange("p c r -> p r c")
                    nc.gpsimd.tensor_copy(hi, src).then_inc(pool_step, 1)
                    done += 1
                    pool.wait_ge(pool_step, done)
                    nc.gpsimd.tensor_tensor(lo, src, hi, ALU.subtract).then_inc(pool_step, 1)
                    done += 1
                    pool.wait_ge(pool_step, done)
                pool.sem_inc(xs_ready, 1)

            for k in range(2):
                normalise(k, k, 16)
            with pool.Fori(0, IMGS) as b:
                with pool.Fori(0, NB // 2) as n2:
                    for k in range(2):
                        t = pool.snap(b * NB + n2 * 2 + k)
                        pool.wait_ge(res_done, t * 3 + (3 + HEAD))
                        pool.dma_start(out[b, :, :, bass.ds(n2 * (2 * BLOCK) + BLOCK * k, BLOCK), :],
                                       ostage[:]).then_inc(out_sem, 16)
                        pool.wait_ge(proj_done, t * PROJ + (AHEAD + NT))
                        normalise(k, t + 2, b * (8 * NB) + n2 * 16 + 32)
                        pool.wait_ge(out_sem, t * 16 + 16)
                        pool.sem_inc(stage_free, 1)
            pool.wait_ge(out_sem, 16 * STRIPS)

        def qview(par, hl, h, c):
            c0 = HALO + 48 * c
            return xs[:, par, hl, h, c0:c0 + 48, HALO:HALO + BLOCK]

        def kview(par, hl, h, c):
            c0 = HALO + KCOLS * c
            return xs[:, par, hl, h, c0:c0 + KCOLS, 0:WIN]

        PASSES = ((0, 0), (0, 1), (1, 0))

        @block.tensor
        def _(pe):
            pe.sem_inc(pv_done, HEAD)
            pe.wait_ge(const_in, N_CONST)
            pe.wait_ge(moments, 1)
            nc.tensor.matmul(fps[:, 0:16], mean8[:], stat[:, 0, :], start=True, stop=True).then_inc(averaged, 1)
            pe.wait_ge(moments, 2)
            nc.tensor.matmul(fps[:, 16:32], mean8[:], stat[:, 1, :], start=True, stop=True).then_inc(averaged, 1)

            def bank_of(p):
                number, bank = p
                if not isinstance(number, int) or number >= 2:
                    pe.wait_ge(proj_lo, number - 1)
                return proj[bank]

            def task(k, g, par, idx):
                kind, c = TASKS[k]
                tps = bank_of(idx)
                if kind == "b":
                    first = True
                    for cls in range(CLASSES):
                        for ws, ms in PASSES:
                            src = qnat[:, c, ms, :]
                            dst = tps[:, 0:CHUNK]
                            if cls < BLOCK:
                                v, o = (a.rearrange("p (m j i) -> p m j i", i=BLOCK, j=BLOCK)[:, :, cls, :]
                                        for a in (src, dst))
                            else:
                                v, o = (a.rearrange("p (a i) -> p a i", i=BLOCK)[:, :, cls - BLOCK]
                                        for a in (src, dst))
                            mm = nc.tensor.matmul(o, r_hl[:, ws, cls, :], v, start=first,
                                                  stop=(cls == CLASSES - 1 and ws == 1), skip_group_check=True)
                            first = False
                else:
                    w = 0 if kind == "q" else 1
                    n = 0
                    for h in range(HALVES):
                        for ws, ms in PASSES:
                            if kind == "q":
                                v, cols = qview(par, ms, h, c), CHUNK
                            else:
                                v, cols = kview(par, ms, h, c), KCOLS * WIN
                            mm = nc.tensor.matmul(tps[:, 0:cols], w_hl[:, w, ws, h, P * g:P * g + P], v,
                                                  start=(n == 0), stop=(n == 5))
                            n += 1
                mm.then_inc(proj_done, 1)

            def values(m, par, idx):
                vps = bank_of(idx)
                n = 0
                for h in range(HALVES):
                    for ws, ms in PASSES:
                        tile = xs[:, par, ws, h, BLOCK * m:BLOCK * m + BLOCK, :].rearrange("p c r -> p (c r)")
                        mm = nc.tensor.matmul(vps[:, 0:CH], tile, w_hl[:, 2, ms, h, :],
                                              start=(n == 0), stop=(n == 5))
                        n += 1
                mm.then_inc(proj_done, 1)

            def score(s, q, half):
                g, m, buf = s // NB, s % NB, s % 2
                if q is not None:
                    pe.wait_ge(exp_done, q - 1)
                if m == 0:
                    pe.wait_ge(proj_lo, half)
                for r in range(PAIRS):
                    o = scores[buf][:, KEYS * r:KEYS * r + KEYS]
                    for n, (ws, ms) in enumerate(PASSES):
                        nc.tensor.matmul(o, qdiag[:, g, ws, m, r, :],
                                         kimg[:, g, ms, BLOCK * m:BLOCK * m + WIN, :],
                                         start=(n == 0), stop=False)
                    for ws in range(2):
                        mm = nc.tensor.matmul(o, bdiag[:, g, ws, m, r, :], onehot[:],
                                              start=False, stop=(ws == 1))
                mm.then_inc(s_done, 1)

            def turn(s, q):
                buf = s % 2
                pe.wait_ge(exp_done, q + 1)
                if not isinstance(q, int) or q >= 2:
                    pe.wait_ge(pt_lo, q - 1 + HEAD)
                for tile in range(2):
                    for r in range(PAIRS):
                        c = (tile * PAIRS + r) * P
                        keys = prob[:, buf, r, BLOCK * tile:BLOCK * tile + BLOCK, :].rearrange("p c r -> p (c r)")
                        mm = nc.tensor.transpose(ptps[buf][:, c:c + P], keys, ident[:])
                mm.then_inc(pt_done, 1)

            def weigh(s, q, par, batches):
                g, m, buf = s // NB, s % NB, s % 2
                pe.wait_ge(pt_lo, q + (1 + HEAD))
                if m % BATCH == 0:
                    pe.wait_ge(o_out, batches)
                for r in range(PAIRS):
                    o = ops[:, (m % BATCH * PAIRS + r) * 64:(m % BATCH * PAIRS + r) * 64 + 64]
                    c = 64 * (PAIRS * g + r)
                    n = 0
                    for tile in range(2):
                        for ws, ms in PASSES:
                            mm = nc.tensor.matmul(o, pt[:, buf, ws, tile, r, :],
                                                  vt[:, par, ms, m + tile, c:c + 64],
                                                  start=(n == 0), stop=(n == 5))
                            n += 1
                mm.then_inc(pv_done, 1)

            def finish(bt, batches, fins):
                pe.wait_ge(o_out, batches)
                pe.wait_ge(res_done, fins)
                for j in range(BATCH):
                    m = BATCH * bt + j
                    mm = nc.tensor.transpose(fps[:, P * j:P * j + P],
                                             osb[:, m, :, :].rearrange("p r d -> p (r d)"), ident[:])
                mm.then_inc(fin_done, 1)

            pe.wait_ge(zeros_set, 5)
            pe.wait_ge(w_lo, 2)
            pe.wait_ge(xs_ready, 1)
            for k in range(NT):
                task(k, 0, 0, (k, k % 2))
            for m in range(VTILES):
                values(m, 0, (NT + m, (NT + m) % 2))
            score(0, None, AHEAD)
            score(1, None, AHEAD)
            turn(0, 0)
            with pe.Fori(0, STRIPS // 2) as t2:
                q0 = pe.snap(t2 * (2 * STEPS))
                p0 = pe.snap(t2 * (2 * PROJ) + AHEAD)
                b0 = pe.snap(t2 * 12)
                f0 = pe.snap(t2 * 6)
                x0 = pe.snap(t2 * 2)
                n = 0
                for k in range(2):
                    for s in range(STEPS):
                        q = q0 + (STEPS * k + s)
                        written = PROJ * k + sum(map(len, PLAN[:max(s - 1, 0)]))
                        score((s + 2) % STEPS, q + 2, p0 + written)
                        turn((s + 1) % STEPS, q + 1)
                        if s == 0:
                            pe.wait_ge(proj_lo, p0 + n)
                        weigh(s, q, k, b0 + (6 * k + s // BATCH + HEAD))
                        if s == VX_STEP:
                            pe.wait_ge(xs_ready, x0 + (k + 2))
                        for what, j in PLAN[s]:
                            p = (p0 + n, (AHEAD + n) % 2)
                            if what == "v":
                                values(j, 1 - k, p)
                            elif s < NB:
                                task(j, 1, k, p)
                            else:
                                task(j, 0, 1 - k, p)
                            n += 1
                        if s in (16, 20):
                            bt = (s - 16) // 4
                            finish(bt, b0 + (6 * k + 4 + bt + HEAD), f0 + (3 * k + bt + HEAD))
                    finish(2, b0 + (6 * k + 6 + HEAD), f0 + (3 * k + 2 + HEAD))

        @block.scalar
        def _(act):
            act.wait_ge(w_scaled, 1)
            nc.scalar.activation(w_hl[:, :, 0, :, :].rearrange("p w h c -> p w (h c)"), wraw, ACT.Copy)\
                .then_inc(w_hi, 1)
            nc.scalar.activation(r_hl[:, 0, :, :], rraw, ACT.Copy).then_inc(w_hi, 1)

            act.wait_ge(moments, 3)
            nc.scalar.activation(stat[:, 5, :], stat[:, 4, :], ACT.Sqrt).then_inc(rooted, 1)

            def task(k, g, p):
                kind, c = TASKS[k]
                tps = proj[p[1]]
                act.wait_ge(proj_done, p[0] + 1)
                if kind == "k":
                    c0 = HALO + KCOLS * c
                    nc.scalar.activation(kimg[:, g, 0, c0:c0 + KCOLS, :],
                                         tps[:, 0:KCOLS * WIN].rearrange("p (c r) -> p c r", r=WIN),
                                         ACT.Copy).then_inc(proj_hi, 1)
                else:
                    dst = qnat if kind == "q" else bnat
                    nc.scalar.activation(dst[:, c, 0, :], tps[:, 0:CHUNK], ACT.Copy).then_inc(proj_hi, 1)

            def values(m, par, p):
                act.wait_ge(proj_done, p[0] + 1)
                nc.scalar.activation(vt[:, par, 0, m, :], proj[p[1]][:, 0:CH], ACT.Copy).then_inc(proj_hi, 1)

            def expo(s, q, batches):
                buf, m = s % 2, s % NB
                act.wait_ge(max_done, q + 1)
                if not isinstance(q, int):
                    act.wait_ge(pt_done, q - 1)
                if batches is not None:
                    act.wait_ge(o_out, batches)
                for r in range(PAIRS):
                    e = nc.scalar.activation(prob[:, buf, r, 0:WIN, 0:WIN],
                                             scores[buf][:, KEYS * r:KEYS * r + KEYS]
                                             .rearrange("p (c r) -> p c r", r=WIN), ACT.Exp, bias=negmax[:, buf, r:r + 1],
                                             accum_out=sums[:, (s // BATCH) % 2, m % BATCH, r:r + 1])
                e.then_inc(exp_done, 1)

            def high(s, q):
                buf = s % 2
                act.wait_ge(pt_done, q + 1)
                if not isinstance(q, int):
                    act.wait_ge(pv_done, q - 1 + HEAD)
                nc.scalar.activation(pt[:, buf, 0, :, :, :].rearrange("p t r c -> p (t r c)"),
                                     ptps[buf][:, :], ACT.Copy).then_inc(pt_hi, 1)

            act.wait_ge(zeros_set, 5)
            act.wait_ge(w_lo, 2)
            for k in range(NT):
                task(k, 0, (k, k % 2))
            for m in range(VTILES):
                values(m, 0, (NT + m, (NT + m) % 2))
            expo(0, 0, None)
            expo(1, 1, None)
            high(0, 0)
            with act.Fori(0, STRIPS // 2) as t2:
                q0 = act.snap(t2 * (2 * STEPS))
                p0 = act.snap(t2 * (2 * PROJ) + AHEAD)
                b0 = act.snap(t2 * 12)
                n = 0
                for k in range(2):
                    for s in range(STEPS):
                        q = q0 + (STEPS * k + s)
                        for what, j in PLAN[s - 1] if s else ():
                            p = (p0 + n, (AHEAD + n) % 2)
                            if what == "v":
                                values(j, 1 - k, p)
                            else:
                                task(j, 1 if s - 1 < NB else 0, p)
                            n += 1
                        high((s + 1) % STEPS, q + 1)
                        new = (s + 2) % BATCH == 0
                        expo((s + 2) % STEPS, q + 2,
                             b0 + (6 * k + (s + 2) // BATCH - 1 + HEAD) if new else None)

        @block.vector
        def _(dve):
            own = [0]

            def settle(ins):
                own[0] += 1
                ins.then_inc(dve_step, 1)
                dve.wait_ge(dve_step, own[0])

            for done in (stat_used, pt_lo, o_out, res_done):
                dve.sem_inc(done, HEAD)
            nc.vector.memset(rraw, 0.0).then_inc(rel_zero, 1)
            dve.wait_ge(const_in, N_CONST)
            dve.wait_ge(rel_zero, 1)
            nc.vector.tensor_scalar(wraw[:, 1, :], wraw[:, 1, :], SCALE, None, ALU.mult).then_inc(w_scaled, 1)
            dve.wait_ge(w_scaled, 1)
            dve.wait_ge(w_hi, 1)
            nc.vector.tensor_tensor(w_hl[:, :, 1, :, :].rearrange("p w h c -> p w (h c)"), wraw,
                                    w_hl[:, :, 0, :, :].rearrange("p w h c -> p w (h c)"), ALU.subtract)\
                .then_inc(w_lo, 1)
            dve.wait_ge(w_hi, 2)
            nc.vector.tensor_tensor(r_hl[:, 1, :, :], rraw, r_hl[:, 0, :, :], ALU.subtract).then_inc(w_lo, 1)

            half = BLOCK * SIDE // 2
            with dve.Fori(0, IMGS) as b:
                for n in range(NB):
                    dve.wait_ge(stat_in[n % 2], b * (8 * NB) + 16 * (n // 2 + 1))
                    for h in range(HALVES):
                        for c in range(2):
                            st = nc.vector.bn_stats(bst[:, h, 2 * n + c, :],
                                                    xraw[:, n % 2, h, half * c:half * c + half])
                    st.then_inc(stat_used, 1)
                dve.wait_ge(stat_used, b * NB + (NB + HEAD))
                dve.sem_inc(passed, 1)
                for h in range(HALVES):
                    st = nc.vector.bn_aggr(mv[:, h, :], bst[:, h, :, :])
                st.then_inc(dve_step, 1)
                dve.wait_ge(dve_step, b * 2 + 1)
                nc.vector.tensor_copy(mvall[:, bass.ds(b, 1), :, :], mv[:].unsqueeze(1)).then_inc(dve_step, 1)
                dve.wait_ge(dve_step, b * 2 + 2)
            own[0] = 2 * IMGS
            means = mvall[:].rearrange("p b h s -> p (b h) s")[:, :, 0]
            varis = mvall[:].rearrange("p b h s -> p (b h) s")[:, :, 1]
            nc.vector.tensor_copy(stat[:, 0, :], means).then_inc(moments, 1)
            dve.wait_ge(averaged, 1)
            settle(nc.vector.tensor_copy(stat[:, 2, :], fps[:, 0:16]))
            settle(nc.vector.tensor_tensor(stat[:, 3, :], means, stat[:, 2, :], ALU.subtract))
            settle(nc.vector.tensor_tensor(stat[:, 3, :], stat[:, 3, :], stat[:, 3, :], ALU.mult))
            nc.vector.tensor_tensor(stat[:, 1, :], varis, stat[:, 3, :], ALU.add).then_inc(moments, 1)
            dve.wait_ge(averaged, 2)
            nc.vector.tensor_scalar(stat[:, 4, :], fps[:, 16:32], EPS, None, ALU.add).then_inc(moments, 1)
            dve.wait_ge(rooted, 1)
            settle(nc.vector.reciprocal(stat[:, 3, :], stat[:, 5, :]))
            settle(nc.vector.tensor_tensor(stat[:, 5, :], stat[:, 3, :], stat[:, 3, :], ALU.mult))
            settle(nc.vector.tensor_tensor(stat[:, 5, :], stat[:, 5, :], stat[:, 4, :], ALU.mult))
            settle(nc.vector.tensor_scalar(stat[:, 5, :], stat[:, 5, :], -0.5, 1.5, ALU.mult, ALU.add))
            settle(nc.vector.tensor_tensor(stat[:, 3, :], stat[:, 3, :], stat[:, 5, :], ALU.mult))
            settle(nc.vector.scalar_tensor_tensor(out=stat[:, 1, :], in0=stat[:, 2, :], scalar=-1.0,
                                                  in1=stat[:, 3, :], op0=ALU.mult, op1=ALU.mult))
            settle(nc.vector.memset(table[:].rearrange("p t e -> p (t e)"), 0.0))
            for b in range(IMGS):
                for e in range(2):
                    src = stat[:, 3 if e == 0 else 1, 2 * b:2 * b + 2]
                    for kind in range(3):
                        dst = table[:, NB * b:NB * b + NB, 4 * kind + e:4 * kind + e + 3:2]
                        first, last = (1 if kind == 0 else 0), (NB - 1 if kind == 2 else NB)
                        settle(nc.vector.tensor_copy(dst[:, first:last, :],
                                                     src.unsqueeze(1).to_broadcast([P, last - first, 2])))
            nc.vector.memset(negmax[:].rearrange("p a b -> p (a b)"), 0.0).then_inc(table_set, 1)
            dve.wait_ge(zeros_set, 5)
            step0 = own[0]
            
            def lo_of(dst, src, hi):
                return nc.vector.tensor_tensor(dst, src, hi, ALU.subtract)

            def task(k, g, p, steps):
                kind, c = TASKS[k]
                tps = proj[p[1]]
                dve.wait_ge(proj_hi, p[0] + 1)
                if kind == "k":
                    c0 = HALO + KCOLS * c
                    lo_of(kimg[:, g, 1, c0:c0 + KCOLS, :],
                          tps[:, 0:KCOLS * WIN].rearrange("p (c r) -> p c r", r=WIN),
                          kimg[:, g, 0, c0:c0 + KCOLS, :]).then_inc(proj_lo, 1)
                    return
                nat, diag = (qnat, qdiag) if kind == "q" else (bnat, bdiag)
                lo_of(nat[:, c, 1, :], tps[:, 0:CHUNK], nat[:, c, 0, :]).then_inc(dve_step, 1)
                dve.wait_ge(dve_step, steps + 1)
                for h in range(4):
                    d0 = DH * h
                    ins = nc.vector.tensor_copy(
                        diag[d0:d0 + DH, g, :, 6 * c:6 * c + 6, h // 2, NQ * (h % 2):NQ * (h % 2) + NQ],
                        nat[d0:d0 + DH, c, :, :].rearrange("p s (m q) -> p s m q", q=NQ))
                ins.then_inc(proj_lo, 1)

            def values(m, par, p):
                dve.wait_ge(proj_hi, p[0] + 1)
                lo_of(vt[:, par, 1, m, :], proj[p[1]][:, 0:CH], vt[:, par, 0, m, :]).then_inc(proj_lo, 1)

            def maxima(s, q):
                buf = s % 2
                dve.wait_ge(s_done, q + 1)
                nc.vector.tensor_reduce(negmax[:, buf, :],
                                        scores[buf][:, 0:PAIRS * KEYS].rearrange("p (r k) -> p r k", r=PAIRS),
                                        axis=AX.X, op=ALU.max, negate=True).then_inc(max_done, 1)

            def low(s, q):
                buf = s % 2
                dve.wait_ge(pt_hi, q + 1)
                lo_of(pt[:, buf, 1, :, :, :].rearrange("p t r c -> p (t r c)"), ptps[buf][:, :],
                      pt[:, buf, 0, :, :, :].rearrange("p t r c -> p (t r c)")).then_inc(pt_lo, 1)

            def outputs(s, q, steps):
                g, bt = s // NB, (s % NB) // BATCH
                dve.wait_ge(pv_done, q + (1 + HEAD))
                nc.vector.reciprocal(rinv[:], sums[:, (s // BATCH) % 2, :, :]).then_inc(dve_step, 1)
                dve.wait_ge(dve_step, steps + 1)
                for half_ in range(2):
                    p0 = NQ * half_
                    src = ops[p0:p0 + NQ, :].rearrange("p (m r c) -> p m r c", m=BATCH, r=PAIRS)[
                        :, :, :, DH * half_:DH * half_ + DH]
                    ins = nc.vector.tensor_tensor(
                        osb[p0:p0 + NQ, BATCH * bt:BATCH * bt + BATCH, PAIRS * g:PAIRS * g + PAIRS, :], src,
                        rinv[p0:p0 + NQ, :, :].unsqueeze(3).to_broadcast([NQ, BATCH, PAIRS, DH]), ALU.mult)
                ins.then_inc(o_out, 1)
                return steps + 1

            def residual(bt, par, idx, stored):
                dve.wait_ge(fin_done, idx + 1)
                if stored is not None:
                    dve.wait_ge(stage_free, stored)
                c0 = BATCH * bt * BLOCK
                for h in range(HALVES):
                    src = fps[:].rearrange("p (m h j i) -> p h i m j", m=BATCH, h=HALVES, j=BLOCK)[:, h]
                    xr = xraw[:, par, h, HALO * SIDE:(HALO + BLOCK) * SIDE]\
                        .rearrange("p (i c) -> p i c", c=SIDE)[:, :, c0:c0 + BATCH * BLOCK]\
                        .rearrange("p i (m j) -> p i m j", j=BLOCK)
                    dst = ostage[:, h, :, c0:c0 + BATCH * BLOCK].rearrange("p i (m j) -> p i m j", j=BLOCK)
                    ins = nc.vector.tensor_tensor(dst, src, xr, ALU.add)
                ins.then_inc(res_done, 1)

            st = step0
            for k in range(NT):
                task(k, 0, (k, k % 2), st)
                st += TASKS[k][0] != "k"
            for m in range(VTILES):
                values(m, 0, (NT + m, (NT + m) % 2))
            maxima(0, 0)
            maxima(1, 1)
            low(0, 0)
            per = 8 + 6
            with dve.Fori(0, STRIPS // 2) as t2:
                q0 = dve.snap(t2 * (2 * STEPS))
                p0 = dve.snap(t2 * (2 * PROJ) + AHEAD)
                d0 = dve.snap(t2 * (2 * per))
                f0 = dve.snap(t2 * 6)
                o0 = dve.snap(t2 * 2)
                n, d = 0, st
                for k in range(2):
                    for s in range(STEPS):
                        q = q0 + (STEPS * k + s)
                        for what, j in PLAN[s - 1] if s else ():
                            p = (p0 + n, (AHEAD + n) % 2)
                            if what == "v":
                                values(j, 1 - k, p)
                            else:
                                task(j, 1 if s - 1 < NB else 0, p, d0 + d)
                                d += TASKS[j][0] != "k"
                            n += 1
                        maxima((s + 2) % STEPS, q + 2)
                        low((s + 1) % STEPS, q + 1)
                        if s % BATCH == BATCH - 1:
                            outputs(s, q, d0 + d)
                            d += 1
                        if s in (17, 21):
                            bt = (s - 17) // 4
                            residual(bt, k, f0 + (3 * k + bt), o0 + (k + HEAD) if bt == 0 else None)
                    residual(2, k, f0 + (3 * k + 2), None)
                    assert n == PROJ * (k + 1) and d == st + per * (k + 1)


def kernel(x, L0_conv_q_weight, L0_conv_kv_weight, L0_conv_height_rel, L0_conv_width_rel):
    import concourse.bacc as bacc
    from concourse.bass_utils import run_bass_kernel_spmd as run

    x = np.asarray(x)
    q_w, kv_w = np.asarray(L0_conv_q_weight), np.asarray(L0_conv_kv_weight)
    h_rel, w_rel = np.asarray(L0_conv_height_rel), np.asarray(L0_conv_width_rel)

    xp = np.zeros((IMGS, P, HALVES, SIDE + 2 * HALO, SIDE), np.float32)
    xp[:, :, :, HALO:HALO + SIDE] = x.reshape(IMGS, 4, 2, DH, SIDE, SIDE).transpose(0, 1, 3, 2, 4, 5)\
        .reshape(IMGS, P, HALVES, SIDE, SIDE)

    def lay(w):
        return np.ascontiguousarray(w.reshape(CH, 4, 2, DH).transpose(1, 3, 2, 0).reshape(P, HALVES, CH))

    kv = kv_w.reshape(HEADS, 2, DH, CH)
    windows = np.arange(WIN)[None, :] + (WIN - 1) - np.arange(BLOCK)[:, None]
    arrays = {
        "x": xp,
        "wq": lay(q_w),
        "wk": lay(kv[:, 0].reshape(CH, CH)),
        "wv": lay(kv[:, 1].reshape(CH, CH)),
        "relw": np.ascontiguousarray(w_rel[windows].transpose(2, 0, 1)),
        "relh": np.ascontiguousarray(h_rel[windows].transpose(2, 0, 1)),
    }
    oh = np.zeros((4, DH, WIN, WIN), np.float16)
    for a in range(WIN):
        oh[:, a, :, a] = 1
        oh[:, WIN + a, a, :] = 1
    arrays["onehot"] = oh.reshape(P, KEYS)
    arrays["ident"] = np.eye(P, dtype=np.float32)
    arrays["mean8"] = np.kron(np.eye(P // 8), np.full((8, 8), 1 / 8)).astype(np.float32)

    nc = bacc.Bacc("TRN2", target_bir_lowering=False, num_devices=1)
    args = [nc.dram_tensor("in_" + n, a.shape, mybir.dt.from_np(a.dtype), kind="ExternalInput").ap()
            for n, a in arrays.items()]
    out = nc.dram_tensor("out_x", (IMGS, P, HALVES, SIDE, SIDE), F32, kind="ExternalOutput").ap()
    build(nc, *args, out)
    r = run(nc, [{"in_" + n: a for n, a in arrays.items()}], core_ids=[0])
    got = r.results[0]["out_x"]
    return np.ascontiguousarray(got.reshape(IMGS, 4, DH, 2, SIDE, SIDE).transpose(0, 1, 3, 2, 4, 5)
                                .reshape(IMGS, CH, SIDE, SIDE))
```

```python
import numpy as np
import concourse.bass as bass
from concourse import mybir
from contextlib import ExitStack

F32 = mybir.dt.float32
F16 = mybir.dt.float16
ACT = mybir.ActivationFunctionType
ALU = mybir.AluOpType
AX = mybir.AxisListType

P = 128
IMGS, CH, SIDE = 8, 256, 96
HEADS, DH = 8, 32
BLOCK, HALO = 8, 3
WIN = BLOCK + 2 * HALO
KEYS = WIN * WIN
NQ = BLOCK * BLOCK
NB = SIDE // BLOCK
STRIPS = IMGS * NB
HALVES = CH // P
GROUPS = 2
PAIRS = 2
STEPS = GROUPS * NB
ROWS = 16
COLS = 104
VTILES = COLS // BLOCK
VITEM = [(0,), (1, 2), (3,), (4,), (5, 6), (7,), (8,), (9,), (10, 11), (12,)]
VITEMS = len(VITEM)
assert sum(VITEM, ()) == tuple(range(VTILES))
CHUNK = 6 * NQ
KCOLS = 32
TASKS = [("q", 0), ("k", 0), ("q", 1), ("k", 1), ("b", 0), ("k", 2), ("b", 1)]
NT = len(TASKS)

NEXT_HALF = NB - 2
PLAN = [[] for _ in range(STEPS)]
for _k in range(NT):
    PLAN[_k].append(("t", _k))
    PLAN[NEXT_HALF + _k].append(("t", _k))
for _v, _step in enumerate((7, 8, 9, 17, 18, 19, 20, 21, 22, 23)):
    PLAN[_step].append(("v", _v))
PROJ = sum(map(len, PLAN))
AHEAD = NT + VITEMS
VX_STEP = NT
assert PROJ == 2 * NT + VITEMS and all(len(step) == 1 for step in PLAN)

BATCH = 4
CLASSES = 2 * BLOCK
SCALE = float(DH) ** -0.5
EPS = 1e-5
NSTAT = 6
TAB = 12


def build(nc, x, wq, wk, wv, relw, relh, onehot_c, ident_c, mean8_c, out):
    ctx = ExitStack()
    with ctx:
        def sb(name, shape, dt):
            return ctx.enter_context(nc.sbuf_tensor(name, shape, dt))

        def pb(name):
            return ctx.enter_context(nc.psum_tensor(name, [P, 512], F32))

        def sem(name):
            return ctx.enter_context(nc.semaphore(name))

        xraw = sb("xraw", [P, 2, HALVES, WIN * SIDE], F32)
        xs = sb("xs", [P, 2, 2, HALVES, COLS, ROWS], F16)
        xn = sb("xn", [P, SIDE, WIN], F32)
        kmix = sb("kmix", [P, GROUPS, PAIRS, COLS, WIN], F16)
        qdiag = sb("qdiag", [P, GROUPS, 2, NB, PAIRS, 2 * NQ], F16)
        bdiag = sb("bdiag", [P, GROUPS, NB, PAIRS, 2 * NQ], F16)
        knat = sb("knat", [P, COLS // KCOLS, 2, KCOLS * WIN], F16)
        vt = sb("vt", [P, 2, 2, VTILES, CH], F16)
        qnat = sb("qnat", [P, 2, 2, CHUNK], F16)
        bnat = sb("bnat", [P, 2, 2, CHUNK], F16)
        prob = sb("prob", [P, 2, PAIRS, ROWS, ROWS], F32)
        pt = sb("pt", [P, 2, 2, 2, PAIRS, P], F16)
        negmax = sb("negmax", [P, 2, PAIRS], F32)
        sums = sb("sums", [P, 2, BATCH, PAIRS], F32)
        rinv = sb("rinv", [P, BATCH, PAIRS], F32)
        osb = sb("osb", [P, NB, GROUPS * PAIRS, DH], F32)
        ostage = sb("ostage", [P, HALVES, BLOCK, SIDE], F32)
        w_hl = sb("w_hl", [P, 3, 2, HALVES, CH], F16)
        r_hl = sb("r_hl", [P, 2, CLASSES, P], F16)
        onehot = sb("onehot", [P, KEYS], F16)
        ident = sb("ident", [P, P], F32)
        mean8 = sb("mean8", [P, P], F32)
        table = sb("table", [P, STRIPS + 2, TAB], F32)
        cur = sb("cur", [P, TAB], F32)
        bst = sb("bst", [P, HALVES, 2 * NB, 6], F32)
        mv = sb("mv", [P, HALVES, 2], F32)
        mvall = sb("mvall", [P, IMGS, HALVES, 2], F32)
        stat = sb("stat", [P, 6, IMGS * HALVES], F32)
        wraw, rraw = (vt[:, k].rearrange("p s m c -> p (s m c)").bitcast(F32)[:, 0:n]
                      for k, n in enumerate((3 * HALVES * CH, CLASSES * P)))
        wraw = wraw.rearrange("p (w c) -> p w c", w=3)
        rraw = rraw.rearrange("p (k c) -> p k c", k=CLASSES)

        scores = [pb("scores0"), pb("scores1")]
        ptps = [pb("ptps0"), pb("ptps1")]
        flat = xs[:].rearrange("p k s h c r -> p (k s h c r)").bitcast(F32)
        ROWS8 = HALVES * BLOCK * SIDE
        chunk = [xraw[:, k, :, 0:BLOCK * SIDE] for k in range(2)]
        chunk += [flat[:, ROWS8 * k:ROWS8 * k + ROWS8].rearrange("p (h c) -> p h c", h=HALVES)
                  for k in range(NSTAT - 2)]
        obank = [pb("obank0"), pb("obank1")]
        proj = [pb("proj0"), pb("proj1")]

        const_in = sem("const_in")
        rel_zero = sem("rel_zero")
        zeros_set = sem("zeros_set")
        stat_in = [sem(f"stat_in{n}") for n in range(NSTAT)]
        stat_used = sem("stat_used")
        w_scaled = sem("w_scaled")
        w_hi = sem("w_hi")
        w_lo = sem("w_lo")
        dve_step = sem("dve_step")
        pool_step = sem("pool_step")
        passed = sem("passed")
        passed_sp = sem("passed_sp")
        moments = sem("moments")
        averaged = sem("averaged")
        rooted = sem("rooted")
        table_set = sem("table_set")
        x_in = [sem("x_in0"), sem("x_in1")]
        xs_ready = sem("xs_ready")
        proj_done = sem("proj_done")
        proj_hi = sem("proj_hi")
        proj_lo = sem("proj_lo")
        moved = [sem(f"moved_{kind}{c}") for kind, c in TASKS]
        diag_done = sem("diag_done")
        s_done = sem("s_done")
        max_done = sem("max_done")
        exp_done = sem("exp_done")
        pt_done = sem("pt_done")
        pt_hi = sem("pt_hi")
        pt_lo = sem("pt_lo")
        pv_done = sem("pv_done")
        o_out = sem("o_out")
        fin_done = sem("fin_done")
        res_done = sem("res_done")
        out_sem = sem("out_sem")
        stage_in = sem("stage_in")

        MOVE = 16 * 2 * PAIRS
        FIRST_BLOCK = {"q": (0, NB // 2), "b": (0, NB // 2),
                       "k": [max(0, (HALO + KCOLS * c - WIN) // BLOCK + 1) if c else 0 for c in range(3)]}
        N_CONST = 16 * (6 + 8)
        ZEROS = 7
        HEAD = 2
        STAT_HEAD = NSTAT
        block = ctx.enter_context(nc.Block())

        @block.sync
        def _(sp):
            for i, w in enumerate((wq, wk, wv)):
                sp.dma_start(wraw[:, i, :], w.rearrange("p h c -> p (h c)")).then_inc(const_in, 16)
            sp.dma_start(onehot[:], onehot_c).then_inc(const_in, 16)
            sp.dma_start(ident[:], ident_c).then_inc(const_in, 16)
            sp.dma_start(mean8[:], mean8_c).then_inc(const_in, 16)
            sp.wait_ge(rel_zero, 1)
            for h in range(4):
                dst = rraw[DH * h:DH * h + DH]
                sp.dma_start(dst[:, 0:BLOCK, DH * h + WIN:DH * h + 2 * WIN], relw).then_inc(const_in, 16)
                sp.dma_start(dst[:, BLOCK:CLASSES, DH * h:DH * h + WIN], relh).then_inc(const_in, 16)

            def load_rows(dst, b, n, row0, rows, done):
                sp.dma_start(dst, x[b, :, :, bass.ds(n * BLOCK + row0, rows), :]
                             .rearrange("p h r w -> p h (r w)")).then_inc(done, 16)

            with sp.Fori(0, IMGS) as b:
                for n in range(NB):
                    sp.wait_ge(stat_used, b * NB + (n + 1 - NSTAT + STAT_HEAD))
                    load_rows(chunk[n % NSTAT], b, n, HALO, BLOCK, stat_in[n % NSTAT])
            sp.wait_ge(stat_used, STRIPS + STAT_HEAD)

            def pieces(g, kind, c):
                for r in range(PAIRS):
                    own, other = slice(64 * r, 64 * r + 64), slice(64 - 64 * r, 128 - 64 * r)
                    if kind == "k":
                        c0 = HALO + KCOLS * c
                        for hl, rows in enumerate((own, other)):
                            yield (kmix[rows, g, r, c0:c0 + KCOLS, :].rearrange("p c r -> p (c r)"),
                                   knat[own, c, hl, :])
                    else:
                        diag, nat = (qdiag[:, g, 0], qnat[:, c, 0]) if kind == "q" else (bdiag[:, g], bnat[:, c, 1])
                        for i in range(2):
                            to, at = other.start + DH * i, own.start + DH * i
                            yield (diag[to:to + DH, 6 * c:6 * c + 6, r, NQ * i:NQ * i + NQ],
                                   nat[at:at + DH].rearrange("p (m q) -> p m q", q=NQ))

            def half_strip(g, numbers):
                for k, number in enumerate(numbers):
                    kind, c = TASKS[k]
                    sp.wait_ge(proj_lo, number + 1)
                    sp.sem_inc(passed_sp, 1)
                    for dst, src in pieces(g, kind, c):
                        sp.dma_start(dst, src).then_inc(moved[k], 16)

            half_strip(0, range(NT))
            order = [(s, item) for s in range(STEPS) for item in PLAN[s]]
            numbers = [n for n, (s, item) in enumerate(order) if item[0] == "t"]
            with sp.Fori(0, STRIPS // 2) as t2:
                p0 = sp.snap(t2 * (2 * PROJ) + AHEAD)
                for k in range(2):
                    half_strip(1, [p0 + (PROJ * k + n) for n in numbers[:NT]])
                    half_strip(0, [p0 + (PROJ * k + n) for n in numbers[NT:]])
            for k in range(NT):
                sp.wait_ge(moved[k], (2 * STRIPS + 1) * MOVE)

        @block.gpsimd
        def _(pool):
            nc.gpsimd.memset(qdiag[:].rearrange("p g s m r q -> p (g s m r q)"), 0.0).then_inc(zeros_set, 1)
            nc.gpsimd.memset(bdiag[:].rearrange("p g m r q -> p (g m r q)"), 0.0).then_inc(zeros_set, 1)
            nc.gpsimd.memset(kmix[:].rearrange("p g s c r -> p (g s c r)"), 0.0).then_inc(zeros_set, 1)
            nc.gpsimd.memset(prob[:].rearrange("p a b c r -> p (a b c r)"), 0.0).then_inc(zeros_set, 1)
            pool.wait_ge(stat_used, STRIPS + STAT_HEAD)
            strips = xs[:].rearrange("p k s h c r -> p (k s h) c r")
            nc.gpsimd.memset(strips[:, :, 0:HALO, :], 0.0).then_inc(zeros_set, 1)
            nc.gpsimd.memset(strips[:, :, HALO + SIDE:COLS, :], 0.0).then_inc(zeros_set, 1)
            nc.gpsimd.memset(strips[:, :, HALO:HALO + SIDE, WIN:ROWS], 0.0).then_inc(zeros_set, 1)
            pool.wait_ge(zeros_set, ZEROS)
            pool.wait_ge(table_set, 1)

            def normalise(par, t, loads):
                pool.wait_ge(x_in[par], loads)
                pool.sem_inc(passed, 1)
                pool.sem_clear(pool_step)
                nc.gpsimd.tensor_copy(cur[:].unsqueeze(1), table[:, t:t + 1, :] if isinstance(t, int) else table[:, bass.ds(t, 1), :]).then_inc(pool_step, 1)
                pool.wait_ge(pool_step, 1)
                done = 1
                for h in range(HALVES):
                    raw = xraw[:, par, h, :].rearrange("p (r c) -> p c r", c=SIDE)
                    for kind, (r0, r1) in enumerate(((0, HALO), (HALO, HALO + BLOCK), (HALO + BLOCK, WIN))):
                        e = 4 * kind + 2 * h
                        nc.gpsimd.tensor_scalar(xn[:, :, r0:r1], raw[:, :, r0:r1],
                                                cur[:, e:e + 1], cur[:, e + 1:e + 2], ALU.mult, ALU.add)\
                            .then_inc(pool_step, 1)
                        done += 1
                    pool.wait_ge(pool_step, done)
                    hi = xs[:, par, 0, h, HALO:HALO + SIDE, 0:WIN]
                    lo = xs[:, par, 1, h, HALO:HALO + SIDE, 0:WIN]
                    nc.gpsimd.tensor_scalar(hi, xn[:], 1.0, None, ALU.mult).then_inc(pool_step, 1)
                    done += 1
                    pool.wait_ge(pool_step, done)
                    nc.gpsimd.tensor_tensor(lo, xn[:], hi, ALU.subtract).then_inc(pool_step, 1)
                    done += 1
                    pool.wait_ge(pool_step, done)
                pool.sem_inc(xs_ready, 1)

            def load_rows(dst, b, n, done):
                pool.dma_start(dst, x[b, :, :, bass.ds(n * BLOCK, WIN), :]
                               .rearrange("p h r w -> p h (r w)")).then_inc(done, 16)

            for k in range(2):
                load_rows(xraw[:, k], 0, k, x_in[k])
            for k in range(2):
                normalise(k, k, 16)

            def strip(k, t, b, n, next_b, next_n):
                centre = xraw[:, k, :, :].rearrange("p h (r c) -> p h r c", c=SIDE)[:, :, HALO:HALO + BLOCK, :]
                pool.dma_start(ostage[:].rearrange("p h r c -> p h (r c)"),
                               centre.rearrange("p h r c -> p h (r c)")).then_inc(stage_in, 16)
                pool.wait_ge(stage_in, t * 16 + 16)
                pool.sem_inc(passed, 1)
                pool.wait_ge(moved[NT - 1], t * (2 * MOVE) + 2 * MOVE)
                pool.sem_inc(passed, 1)
                load_rows(xraw[:, k], next_b, next_n, x_in[k])
                normalise(k, t + 2, (t - k) * 8 + 32)
                pool.wait_ge(res_done, t * 3 + (3 + HEAD))
                pool.sem_inc(passed, 1)
                pool.dma_start(out[b, :, :, bass.ds(n * BLOCK, BLOCK), :], ostage[:]).then_inc(out_sem, 16)
                pool.wait_ge(out_sem, t * 16 + 16)
                pool.sem_inc(passed, 1)

            def image(b, next_b):
                with pool.Fori(0, NB // 2 - 1) as n2:
                    for k in range(2):
                        strip(k, pool.snap(n2 * 2 + b * NB + k), b, n2 * 2 + k, b, n2 * 2 + (k + 2))
                for k in range(2):
                    t = b * NB + (NB - 2 + k)
                    strip(k, t if isinstance(t, int) else pool.snap(t), b, NB - 2 + k, next_b, k)

            with pool.Fori(0, IMGS - 1) as b:
                image(b, b + 1)
            image(IMGS - 1, 0)

        def qview(par, hl, h, c):
            c0 = HALO + 48 * c
            return xs[:, par, hl, h, c0:c0 + 48, HALO:HALO + BLOCK]

        def kview(par, hl, h, c):
            c0 = HALO + KCOLS * c
            return xs[:, par, hl, h, c0:c0 + KCOLS, 0:WIN]

        PASSES = ((0, 0), (0, 1), (1, 0))

        @block.tensor
        def _(pe):
            pe.sem_inc(pv_done, HEAD)
            pe.wait_ge(const_in, N_CONST)
            pe.wait_ge(moments, 1)
            nc.tensor.matmul(obank[0][:, 0:16], mean8[:], stat[:, 0, :], start=True, stop=True).then_inc(averaged, 1)
            pe.wait_ge(moments, 2)
            nc.tensor.matmul(obank[0][:, 16:32], mean8[:], stat[:, 1, :], start=True, stop=True).then_inc(averaged, 1)

            def bank_of(p):
                number, bank = p
                if not isinstance(number, int) or number >= 2:
                    pe.wait_ge(proj_lo, number - 1)
                return proj[bank]

            def task(k, g, par, idx):
                kind, c = TASKS[k]
                tps = bank_of(idx)
                if kind == "b":
                    first = True
                    for cls in range(CLASSES):
                        for ws, ms in PASSES:
                            src = qnat[:, c, ms, :]
                            dst = tps[:, 0:CHUNK]
                            if cls < BLOCK:
                                v, o = (a.rearrange("p (m j i) -> p m j i", i=BLOCK, j=BLOCK)[:, :, cls, :]
                                        for a in (src, dst))
                            else:
                                v, o = (a.rearrange("p (a i) -> p a i", i=BLOCK)[:, :, cls - BLOCK]
                                        for a in (src, dst))
                            mm = nc.tensor.matmul(o, r_hl[:, ws, cls, :], v, start=first,
                                                  stop=(cls == CLASSES - 1 and ws == 1), skip_group_check=True)
                            first = False
                else:
                    w = 0 if kind == "q" else 1
                    n = 0
                    for h in range(HALVES):
                        for ws, ms in PASSES:
                            if kind == "q":
                                v, cols = qview(par, ms, h, c), CHUNK
                            else:
                                v, cols = kview(par, ms, h, c), KCOLS * WIN
                            mm = nc.tensor.matmul(tps[:, 0:cols], w_hl[:, w, ws, h, P * g:P * g + P], v,
                                                  start=(n == 0), stop=(n == 5))
                            n += 1
                mm.then_inc(proj_done, 1)

            def values(item, par, idx):
                vps = bank_of(idx)
                for i, m in enumerate(VITEM[item]):
                    n = 0
                    for h in range(HALVES):
                        for ws, ms in PASSES:
                            tile = xs[:, par, ws, h, BLOCK * m:BLOCK * m + BLOCK, :].rearrange("p c r -> p (c r)")
                            mm = nc.tensor.matmul(vps[:, CH * i:CH * i + CH], tile, w_hl[:, 2, ms, h, :],
                                                  start=(n == 0), stop=(n == 5))
                            n += 1
                mm.then_inc(proj_done, 1)

            def score(s, q, half):
                g, m, buf = s // NB, s % NB, s % 2
                if q is not None:
                    pe.wait_ge(exp_done, q - 1)
                for k, (kind, c) in enumerate(TASKS):
                    if m == FIRST_BLOCK[kind][c]:
                        pe.wait_ge(moved[k], half * MOVE)
                if m in FIRST_BLOCK["b"]:
                    pe.wait_ge(diag_done, half * 4 - (1 if m == 0 else 0))
                for r in range(PAIRS):
                    o = scores[buf][:, KEYS * r:KEYS * r + KEYS]
                    keys = kmix[:, g, r, BLOCK * m:BLOCK * m + WIN, :]
                    nc.tensor.matmul(o, qdiag[:, g, 0, m, r, :], keys, start=True, stop=False)
                    nc.tensor.matmul(o, qdiag[:, g, 1, m, r, :], keys, start=False, stop=False)
                    mm = nc.tensor.matmul(o, bdiag[:, g, m, r, :], onehot[:], start=False, stop=True)
                mm.then_inc(s_done, 1)

            def turn(s, q):
                buf = s % 2
                pe.wait_ge(exp_done, q + 1)
                if not isinstance(q, int) or q >= 2:
                    pe.wait_ge(pt_lo, q - 1 + HEAD)
                for tile in range(2):
                    for r in range(PAIRS):
                        c = (tile * PAIRS + r) * P
                        keys = prob[:, buf, r, BLOCK * tile:BLOCK * tile + BLOCK, :].rearrange("p c r -> p (c r)")
                        mm = nc.tensor.transpose(ptps[buf][:, c:c + P], keys, ident[:])
                mm.then_inc(pt_done, 1)

            def weigh(s, q, par, batches, fins):
                g, m, buf = s // NB, s % NB, s % 2
                pe.wait_ge(pt_lo, q + (1 + HEAD))
                ops = obank[(s // BATCH) % 2]
                if m % BATCH == 0:
                    pe.wait_ge(o_out, batches)
                    if fins is not None:
                        pe.wait_ge(res_done, fins)
                for r in range(PAIRS):
                    o = ops[:, (m % BATCH * PAIRS + r) * 64:(m % BATCH * PAIRS + r) * 64 + 64]
                    c = 64 * (PAIRS * g + r)
                    n = 0
                    for tile in range(2):
                        for ws, ms in PASSES:
                            mm = nc.tensor.matmul(o, pt[:, buf, ws, tile, r, :],
                                                  vt[:, par, ms, m + tile, c:c + 64],
                                                  start=(n == 0), stop=(n == 5))
                            n += 1
                mm.then_inc(pv_done, 1)

            def finish(bt, batches):
                fps = obank[(bt + 3) % 2]
                pe.wait_ge(o_out, batches)
                for j in range(BATCH):
                    m = BATCH * bt + j
                    mm = nc.tensor.transpose(fps[:, P * j:P * j + P],
                                             osb[:, m, :, :].rearrange("p r d -> p (r d)"), ident[:])
                mm.then_inc(fin_done, 1)

            pe.wait_ge(zeros_set, ZEROS)
            pe.wait_ge(w_lo, 2)
            pe.wait_ge(xs_ready, 1)
            for k in range(NT):
                task(k, 0, 0, (k, k % 2))
            for m in range(VITEMS):
                values(m, 0, (NT + m, (NT + m) % 2))
            score(0, None, 1)
            score(1, None, 1)
            turn(0, 0)
            with pe.Fori(0, STRIPS // 2) as t2:
                q0 = pe.snap(t2 * (2 * STEPS))
                p0 = pe.snap(t2 * (2 * PROJ) + AHEAD)
                b0 = pe.snap(t2 * 12)
                f0 = pe.snap(t2 * 6)
                x0 = pe.snap(t2 * 2)
                g0 = pe.snap(t2 * 4)
                n = 0
                for k in range(2):
                    for s in range(STEPS):
                        q = q0 + (STEPS * k + s)
                        score((s + 2) % STEPS, q + 2, g0 + (2 * k + 1 + (s + 2) // NB))
                        turn((s + 1) % STEPS, q + 1)
                        if s == 0:
                            pe.wait_ge(proj_lo, p0 + (n - 1))
                            values_ready = p0 + n
                        if s == BATCH:
                            pe.wait_ge(proj_lo, values_ready)
                        turned = {5: 1, 0: -1, 1: 0}.get(s // BATCH)
                        weigh(s, q, k, b0 + (6 * k + s // BATCH - 1 + HEAD),
                              None if turned is None else f0 + (3 * k + turned + HEAD))
                        if s == VX_STEP:
                            pe.wait_ge(xs_ready, x0 + (k + 2))
                        for what, j in PLAN[s]:
                            p = (p0 + n, (AHEAD + n) % 2)
                            if what == "v":
                                values(j, 1 - k, p)
                            elif s < NEXT_HALF:
                                task(j, 1, k, p)
                            else:
                                task(j, 0, 1 - k, p)
                            n += 1
                        if s in (16, 20):
                            bt = (s - 16) // 4
                            finish(bt, b0 + (6 * k + 4 + bt + HEAD))
                    finish(2, b0 + (6 * k + 6 + HEAD))

        @block.scalar
        def _(act):
            act.wait_ge(w_scaled, 1)
            nc.scalar.activation(w_hl[:, :, 0, :, :].rearrange("p w h c -> p w (h c)"), wraw, ACT.Copy)\
                .then_inc(w_hi, 1)
            nc.scalar.activation(r_hl[:, 0, :, :], rraw, ACT.Copy).then_inc(w_hi, 1)

            act.wait_ge(moments, 3)
            nc.scalar.activation(stat[:, 5, :], stat[:, 4, :], ACT.Sqrt).then_inc(rooted, 1)

            def task(k, p, halves):
                kind, c = TASKS[k]
                tps = proj[p[1]]
                act.wait_ge(proj_done, p[0] + 1)
                if not isinstance(halves, int):
                    act.wait_ge(moved[k], halves * MOVE)
                if kind == "k":
                    nc.scalar.activation(knat[:, c, 0, :], tps[:, 0:KCOLS * WIN], ACT.Copy).then_inc(proj_hi, 1)
                else:
                    dst = qnat if kind == "q" else bnat
                    nc.scalar.activation(dst[:, c, 0, :], tps[:, 0:CHUNK], ACT.Copy).then_inc(proj_hi, 1)

            def values(item, par, p):
                m, n = VITEM[item][0], len(VITEM[item])
                act.wait_ge(proj_done, p[0] + 1)
                nc.scalar.activation(vt[:, par, 0, m:m + n, :].rearrange("p m c -> p (m c)"),
                                     proj[p[1]][:, 0:n * CH], ACT.Copy).then_inc(proj_hi, 1)

            def expo(s, q, batches):
                buf, m = s % 2, s % NB
                act.wait_ge(max_done, q + 1)
                if not isinstance(q, int):
                    act.wait_ge(pt_done, q - 1)
                if batches is not None:
                    act.wait_ge(o_out, batches)
                for r in range(PAIRS):
                    e = nc.scalar.activation(prob[:, buf, r, 0:WIN, 0:WIN],
                                             scores[buf][:, KEYS * r:KEYS * r + KEYS]
                                             .rearrange("p (c r) -> p c r", r=WIN), ACT.Exp, bias=negmax[:, buf, r:r + 1],
                                             accum_out=sums[:, (s // BATCH) % 2, m % BATCH, r:r + 1])
                e.then_inc(exp_done, 1)

            def high(s, q):
                buf = s % 2
                act.wait_ge(pt_done, q + 1)
                if not isinstance(q, int):
                    act.wait_ge(pv_done, q - 1 + HEAD)
                nc.scalar.activation(pt[:, buf, 0, :, :, :].rearrange("p t r c -> p (t r c)"),
                                     ptps[buf][:, :], ACT.Copy).then_inc(pt_hi, 1)

            act.wait_ge(zeros_set, ZEROS)
            act.wait_ge(w_lo, 2)
            for k in range(NT):
                task(k, (k, k % 2), 0)
            for m in range(VITEMS):
                values(m, 0, (NT + m, (NT + m) % 2))
            expo(0, 0, None)
            expo(1, 1, None)
            high(0, 0)
            with act.Fori(0, STRIPS // 2) as t2:
                q0 = act.snap(t2 * (2 * STEPS))
                p0 = act.snap(t2 * (2 * PROJ) + AHEAD)
                h0 = act.snap(t2 * 4 + 1)
                b0 = act.snap(t2 * 12)
                n = 0
                for k in range(2):
                    for s in range(STEPS):
                        q = q0 + (STEPS * k + s)
                        for what, j in PLAN[s - 1] if s else ():
                            p = (p0 + n, (AHEAD + n) % 2)
                            if what == "v":
                                values(j, 1 - k, p)
                            else:
                                task(j, p, h0 + (2 * k + (s - 1 >= NEXT_HALF)))
                            n += 1
                        high((s + 1) % STEPS, q + 1)
                        new = (s + 2) % BATCH == 0
                        expo((s + 2) % STEPS, q + 2,
                             b0 + (6 * k + (s + 2) // BATCH - 1 + HEAD) if new else None)
                    for what, j in PLAN[STEPS - 1]:
                        values(j, 1 - k, (p0 + n, (AHEAD + n) % 2))
                        n += 1

        @block.vector
        def _(dve):
            own = [0]

            def settle(ins):
                own[0] += 1
                ins.then_inc(dve_step, 1)
                dve.wait_ge(dve_step, own[0])

            dve.sem_inc(stat_used, STAT_HEAD)
            for done in (pt_lo, o_out, res_done):
                dve.sem_inc(done, HEAD)
            nc.vector.memset(rraw, 0.0).then_inc(rel_zero, 1)
            dve.wait_ge(const_in, N_CONST)
            dve.wait_ge(rel_zero, 1)
            nc.vector.tensor_scalar(wraw[:, 1, :], wraw[:, 1, :], SCALE, None, ALU.mult).then_inc(w_scaled, 1)
            dve.wait_ge(w_scaled, 1)
            dve.wait_ge(w_hi, 1)
            nc.vector.tensor_tensor(w_hl[:, :, 1, :, :].rearrange("p w h c -> p w (h c)"), wraw,
                                    w_hl[:, :, 0, :, :].rearrange("p w h c -> p w (h c)"), ALU.subtract)\
                .then_inc(w_lo, 1)
            dve.wait_ge(w_hi, 2)
            nc.vector.tensor_tensor(r_hl[:, 1, :, :], rraw, r_hl[:, 0, :, :], ALU.subtract).then_inc(w_lo, 1)

            half = BLOCK * SIDE // 2
            with dve.Fori(0, IMGS) as b:
                for n in range(NB):
                    dve.wait_ge(stat_in[n % NSTAT], b * (16 * NB // NSTAT) + 16 * (n // NSTAT + 1))
                    for h in range(HALVES):
                        for c in range(2):
                            st = nc.vector.bn_stats(bst[:, h, 2 * n + c, :],
                                                    chunk[n % NSTAT][:, h, half * c:half * c + half])
                    st.then_inc(stat_used, 1)
                dve.wait_ge(stat_used, b * NB + (NB + STAT_HEAD))
                dve.sem_inc(passed, 1)
                for h in range(HALVES):
                    st = nc.vector.bn_aggr(mv[:, h, :], bst[:, h, :, :])
                st.then_inc(dve_step, 1)
                dve.wait_ge(dve_step, b * 2 + 1)
                nc.vector.tensor_copy(mvall[:, bass.ds(b, 1), :, :], mv[:].unsqueeze(1)).then_inc(dve_step, 1)
                dve.wait_ge(dve_step, b * 2 + 2)
            own[0] = 2 * IMGS
            means = mvall[:].rearrange("p b h s -> p (b h) s")[:, :, 0]
            varis = mvall[:].rearrange("p b h s -> p (b h) s")[:, :, 1]
            nc.vector.tensor_copy(stat[:, 0, :], means).then_inc(moments, 1)
            dve.wait_ge(averaged, 1)
            settle(nc.vector.tensor_copy(stat[:, 2, :], obank[0][:, 0:16]))
            settle(nc.vector.tensor_tensor(stat[:, 3, :], means, stat[:, 2, :], ALU.subtract))
            settle(nc.vector.tensor_tensor(stat[:, 3, :], stat[:, 3, :], stat[:, 3, :], ALU.mult))
            nc.vector.tensor_tensor(stat[:, 1, :], varis, stat[:, 3, :], ALU.add).then_inc(moments, 1)
            dve.wait_ge(averaged, 2)
            nc.vector.tensor_scalar(stat[:, 4, :], obank[0][:, 16:32], EPS, None, ALU.add).then_inc(moments, 1)
            dve.wait_ge(rooted, 1)
            settle(nc.vector.reciprocal(stat[:, 3, :], stat[:, 5, :]))
            settle(nc.vector.tensor_tensor(stat[:, 5, :], stat[:, 3, :], stat[:, 3, :], ALU.mult))
            settle(nc.vector.tensor_tensor(stat[:, 5, :], stat[:, 5, :], stat[:, 4, :], ALU.mult))
            settle(nc.vector.tensor_scalar(stat[:, 5, :], stat[:, 5, :], -0.5, 1.5, ALU.mult, ALU.add))
            settle(nc.vector.tensor_tensor(stat[:, 3, :], stat[:, 3, :], stat[:, 5, :], ALU.mult))
            settle(nc.vector.scalar_tensor_tensor(out=stat[:, 1, :], in0=stat[:, 2, :], scalar=-1.0,
                                                  in1=stat[:, 3, :], op0=ALU.mult, op1=ALU.mult))
            settle(nc.vector.memset(table[:].rearrange("p t e -> p (t e)"), 0.0))
            for b in range(IMGS):
                for e in range(2):
                    src = stat[:, 3 if e == 0 else 1, 2 * b:2 * b + 2]
                    for kind in range(3):
                        dst = table[:, NB * b:NB * b + NB, 4 * kind + e:4 * kind + e + 3:2]
                        first, last = (1 if kind == 0 else 0), (NB - 1 if kind == 2 else NB)
                        settle(nc.vector.tensor_copy(dst[:, first:last, :],
                                                     src.unsqueeze(1).to_broadcast([P, last - first, 2])))
            nc.vector.memset(negmax[:].rearrange("p a b -> p (a b)"), 0.0).then_inc(table_set, 1)
            dve.wait_ge(zeros_set, ZEROS)
            step0 = own[0]

            def lo_of(dst, src, hi):
                return nc.vector.tensor_tensor(dst, src, hi, ALU.subtract)

            def task(k, p):
                kind, c = TASKS[k]
                dve.wait_ge(proj_hi, p[0] + 1)
                if kind == "k":
                    lo_of(knat[:, c, 1, :], proj[p[1]][:, 0:KCOLS * WIN], knat[:, c, 0, :]).then_inc(proj_lo, 1)
                else:
                    nat = qnat if kind == "q" else bnat
                    lo_of(nat[:, c, 1, :], proj[p[1]][:, 0:CHUNK], nat[:, c, 0, :]).then_inc(proj_lo, 1)

            def diagonal(k, g, p):
                kind, c = TASKS[k]
                if kind == "q":
                    dve.wait_ge(proj_lo, p[0] + 1)
                for h in range(4):
                    d0 = DH * h
                    place = (slice(6 * c, 6 * c + 6), h // 2, slice(NQ * (h % 2), NQ * (h % 2) + NQ))
                    if kind == "q":
                        ins = nc.vector.tensor_copy(
                            qdiag[d0:d0 + DH, g, :, place[0], place[1], place[2]],
                            qnat[d0:d0 + DH, c].rearrange("p s (m q) -> p s m q", q=NQ))
                    elif kind == "b":
                        ins = nc.vector.tensor_copy(
                            bdiag[d0:d0 + DH, g, place[0], place[1], place[2]],
                            bnat[d0:d0 + DH, c, 0].rearrange("p (m q) -> p m q", q=NQ))
                if kind != "k":
                    ins.then_inc(diag_done, 1)

            def values(item, par, p):
                m, n = VITEM[item][0], len(VITEM[item])
                hi, lo = (vt[:, par, hl, m:m + n, :].rearrange("p m c -> p (m c)") for hl in range(2))
                dve.wait_ge(proj_hi, p[0] + 1)
                lo_of(lo, proj[p[1]][:, 0:n * CH], hi).then_inc(proj_lo, 1)

            def maxima(s, q):
                buf = s % 2
                dve.wait_ge(s_done, q + 1)
                nc.vector.tensor_reduce(negmax[:, buf, :],
                                        scores[buf][:, 0:PAIRS * KEYS].rearrange("p (r k) -> p r k", r=PAIRS),
                                        axis=AX.X, op=ALU.max, negate=True).then_inc(max_done, 1)

            def low(s, q):
                buf = s % 2
                dve.wait_ge(pt_hi, q + 1)
                lo_of(pt[:, buf, 1, :, :, :].rearrange("p t r c -> p (t r c)"), ptps[buf][:, :],
                      pt[:, buf, 0, :, :, :].rearrange("p t r c -> p (t r c)")).then_inc(pt_lo, 1)

            def outputs(s, q, steps):
                g, bt = s // NB, (s % NB) // BATCH
                dve.wait_ge(pv_done, q + (1 + HEAD))
                nc.vector.reciprocal(rinv[:], sums[:, (s // BATCH) % 2, :, :]).then_inc(dve_step, 1)
                dve.wait_ge(dve_step, steps + 1)
                for half_ in range(2):
                    p0 = NQ * half_
                    src = obank[(s // BATCH) % 2][p0:p0 + NQ, :].rearrange("p (m r c) -> p m r c", m=BATCH, r=PAIRS)[
                        :, :, :, DH * half_:DH * half_ + DH]
                    ins = nc.vector.tensor_tensor(
                        osb[p0:p0 + NQ, BATCH * bt:BATCH * bt + BATCH, PAIRS * g:PAIRS * g + PAIRS, :], src,
                        rinv[p0:p0 + NQ, :, :].unsqueeze(3).to_broadcast([NQ, BATCH, PAIRS, DH]), ALU.mult)
                ins.then_inc(o_out, 1)
                return steps + 1

            def residual(bt, idx, staged):
                dve.wait_ge(fin_done, idx + 1)
                if staged is not None:
                    dve.wait_ge(stage_in, staged)
                c0 = BATCH * bt * BLOCK
                for h in range(HALVES):
                    src = obank[(bt + 3) % 2][:].rearrange("p (m h j i) -> p h i m j", m=BATCH, h=HALVES, j=BLOCK)[:, h]
                    dst = ostage[:, h, :, c0:c0 + BATCH * BLOCK].rearrange("p i (m j) -> p i m j", j=BLOCK)
                    ins = nc.vector.tensor_tensor(dst, src, dst, ALU.add)
                ins.then_inc(res_done, 1)

            for k in range(NT):
                task(k, (k, k % 2))
                diagonal(k, 0, (k, k % 2))
            for m in range(VITEMS):
                values(m, 0, (NT + m, (NT + m) % 2))
            maxima(0, 0)
            maxima(1, 1)
            low(0, 0)
            per = 6
            with dve.Fori(0, STRIPS // 2) as t2:
                q0 = dve.snap(t2 * (2 * STEPS))
                p0 = dve.snap(t2 * (2 * PROJ) + AHEAD)
                d0 = dve.snap(t2 * (2 * per) + step0)
                f0 = dve.snap(t2 * 6)
                o0 = dve.snap(t2 * 32)
                n, d = 0, 0
                for k in range(2):
                    for s in range(STEPS):
                        q = q0 + (STEPS * k + s)
                        maxima((s + 2) % STEPS, q + 2)
                        for what, j in PLAN[s - 1] if s else ():
                            p = (p0 + n, (AHEAD + n) % 2)
                            if what == "v":
                                values(j, 1 - k, p)
                            else:
                                task(j, p)
                            n += 1
                        if s != STEPS - 1:
                            low((s + 1) % STEPS, q + 1)
                        for what, j in PLAN[s - 1] if s else ():
                            if what == "t":
                                diagonal(j, 1 if s - 1 < NEXT_HALF else 0, p)
                        if s % BATCH == BATCH - 1:
                            outputs(s, q, d0 + d)
                            d += 1
                        if s == STEPS - 1:
                            low((s + 1) % STEPS, q + 1)
                        if s in (17, 21):
                            bt = (s - 17) // 4
                            residual(bt, f0 + (3 * k + bt), o0 + (16 * k + 16) if bt == 0 else None)
                    for what, j in PLAN[STEPS - 1]:
                        values(j, 1 - k, (p0 + n, (AHEAD + n) % 2))
                        n += 1
                    residual(2, f0 + (3 * k + 2), None)
                    assert n == PROJ * (k + 1) and d == per * (k + 1)


def kernel(x, L0_conv_q_weight, L0_conv_kv_weight, L0_conv_height_rel, L0_conv_width_rel):
    import concourse.bacc as bacc
    from concourse.bass_utils import run_bass_kernel_spmd as run

    x = np.asarray(x)
    q_w, kv_w = np.asarray(L0_conv_q_weight), np.asarray(L0_conv_kv_weight)
    h_rel, w_rel = np.asarray(L0_conv_height_rel), np.asarray(L0_conv_width_rel)

    xp = np.zeros((IMGS, P, HALVES, SIDE + 2 * HALO, SIDE), np.float32)
    xp[:, :, :, HALO:HALO + SIDE] = x.reshape(IMGS, 4, 2, DH, SIDE, SIDE).transpose(0, 1, 3, 2, 4, 5)\
        .reshape(IMGS, P, HALVES, SIDE, SIDE)

    def lay(w):
        return np.ascontiguousarray(w.reshape(CH, 4, 2, DH).transpose(1, 3, 2, 0).reshape(P, HALVES, CH))

    kv = kv_w.reshape(HEADS, 2, DH, CH)
    windows = np.arange(WIN)[None, :] + (WIN - 1) - np.arange(BLOCK)[:, None]
    arrays = {
        "x": xp,
        "wq": lay(q_w),
        "wk": lay(kv[:, 0].reshape(CH, CH)),
        "wv": lay(kv[:, 1].reshape(CH, CH)),
        "relw": np.ascontiguousarray(w_rel[windows].transpose(2, 0, 1)),
        "relh": np.ascontiguousarray(h_rel[windows].transpose(2, 0, 1)),
    }
    oh = np.zeros((4, DH, WIN, WIN), np.float16)
    for a in range(WIN):
        oh[:, a, :, a] = 1
        oh[:, WIN + a, a, :] = 1
    arrays["onehot"] = oh.reshape(P, KEYS)
    arrays["ident"] = np.eye(P, dtype=np.float32)
    arrays["mean8"] = np.kron(np.eye(P // 8), np.full((8, 8), 1 / 8)).astype(np.float32)

    nc = bacc.Bacc("TRN2", target_bir_lowering=False, num_devices=1)
    args = [nc.dram_tensor("in_" + n, a.shape, mybir.dt.from_np(a.dtype), kind="ExternalInput").ap()
            for n, a in arrays.items()]
    out = nc.dram_tensor("out_x", (IMGS, P, HALVES, SIDE, SIDE), F32, kind="ExternalOutput").ap()
    build(nc, *args, out)
    r = run(nc, [{"in_" + n: a for n, a in arrays.items()}], core_ids=[0])
    got = r.results[0]["out_x"]
    return np.ascontiguousarray(got.reshape(IMGS, 4, DH, 2, SIDE, SIDE).transpose(0, 1, 3, 2, 4, 5)
                                .reshape(IMGS, CH, SIDE, SIDE))
```
